# Optimizing a Trainium2 kernel written in Bass

```python
import numpy as np
import jax
import jax.numpy as jnp

def _softmax(x, axis=-1):
    return jax.nn.softmax(x, axis=axis)

def _gelu(x):
    return jax.nn.gelu(x, approximate=True)

def _silu(x):
    return jax.nn.silu(x)

def _sigmoid(x):
    return jax.nn.sigmoid(x)

def _layernorm(x, axis=-1, eps=1e-05):
    m = jnp.mean(x, axis=axis, keepdims=True)
    v = jnp.var(x, axis=axis, keepdims=True)
    return (x - m) / jnp.sqrt(v + eps)

def _scatter_add(tgt, idx, src, axis=0):
    return tgt.at[idx].add(src)

def _segment_sum(src, seg, n):
    return jax.ops.segment_sum(src, seg, n)
kernel_name = 'mk_conv_preact_d4_conv_nchw512_r2_dc5b54'

def setup_inputs(seed: int=0):
    np.random.seed(seed)
    _w = jnp.asarray

    def _rec_inputs():
        import jax
        import jax.numpy as jnp
        _gk = jax.random.key(seed)
        x = -0.0002091 + 1 * jax.random.normal(jax.random.fold_in(_gk, 1), (32, 256, 28, 28), jnp.float32)
        return x
    x = _rec_inputs()

    def _L0_conv_setup():
        import jax, jax.numpy as jnp
        import numpy as np
        STRIDE = 1

        def sparsemax(z):
            K = z.shape[-1]
            zs = -jnp.sort(-z, axis=-1)
            cum = jnp.cumsum(zs, axis=-1)
            ks = jnp.arange(1, K + 1, dtype=z.dtype)
            support = 1 + ks * zs > cum
            k_z = jnp.sum(support, axis=-1, keepdims=True)
            cum_k = jnp.take_along_axis(cum, k_z - 1, axis=-1)
            tau = (cum_k - 1) / k_z.astype(z.dtype)
            return jnp.maximum(z - tau, 0)
        key = jax.random.key(seed)
        k1, k2, k3, k4 = jax.random.split(key, 4)
        B, Cin, Cout, H, W, K = (32, 256, 256, 28, 28, 8)
        x = jax.random.normal(k1, (B, Cin, H, W), dtype=jnp.float32)
        gate_w = jax.random.normal(k2, (K, Cin), dtype=jnp.float32) * 0.02
        gate_b = jax.random.normal(k3, (K,), dtype=jnp.float32) * 0.02
        expert_w = jax.random.normal(k4, (K, Cout, Cin), dtype=jnp.float32) * 0.02
        return {'x': x, 'gate_w': gate_w, 'gate_b': gate_b, 'expert_w': expert_w}
    _L0_conv_all = _L0_conv_setup()
    _L0_conv_in = {k: v for k, v in _L0_conv_all.items() if k in ('gate_w', 'gate_b', 'expert_w')}
    del _L0_conv_all

    def _L1_conv_setup():
        import jax, jax.numpy as jnp
        import numpy as np
        from jax import lax
        EPS = 1e-05
        DW_THRESH = 4.0
        PW_THRESH = 0.001
        C_IN = 256
        C_OUT = 256

        def _bn(x, g, b, m, v):
            inv = g * lax.rsqrt(v + EPS)
            return x * inv[None, :, None, None] + (b - m * inv)[None, :, None, None]

        def _prune(x, thresh):
            amax = jnp.max(jnp.abs(x), axis=(2, 3), keepdims=True)
            return jnp.where(amax < thresh, jnp.zeros_like(x), x)
        key = jax.random.key(seed)
        ks = jax.random.split(key, 8)
        B, H, W = (32, 28, 28)
        x = jax.random.normal(ks[0], (B, C_IN, H, W), dtype=jnp.float32)
        dw_w = jax.random.normal(ks[1], (C_IN, 1, 3, 3), dtype=jnp.float32) * 0.1
        dw_b = jax.random.normal(ks[2], (C_IN,), dtype=jnp.float32) * 0.1
        bn1_g = jnp.ones((C_IN,), jnp.float32)
        bn1_b = jnp.zeros((C_IN,), jnp.float32)
        bn1_m = jnp.zeros((C_IN,), jnp.float32)
        bn1_v = jnp.ones((C_IN,), jnp.float32)
        pw_w = jax.random.normal(ks[3], (C_OUT, C_IN, 1, 1), dtype=jnp.float32) * 0.05
        pw_b = jax.random.normal(ks[4], (C_OUT,), dtype=jnp.float32) * 0.1
        bn2_g = jnp.ones((C_OUT,), jnp.float32)
        bn2_b = jnp.zeros((C_OUT,), jnp.float32)
        bn2_m = jnp.zeros((C_OUT,), jnp.float32)
        bn2_v = jnp.ones((C_OUT,), jnp.float32)
        return dict(x=x, dw_w=dw_w, dw_b=dw_b, bn1_g=bn1_g, bn1_b=bn1_b, bn1_m=bn1_m, bn1_v=bn1_v, pw_w=pw_w, pw_b=pw_b, bn2_g=bn2_g, bn2_b=bn2_b, bn2_m=bn2_m, bn2_v=bn2_v)
    _L1_conv_all = _L1_conv_setup()
    _L1_conv_in = {k: v for k, v in _L1_conv_all.items() if k in ('dw_w', 'dw_b', 'bn1_g', 'bn1_b', 'bn1_m', 'bn1_v', 'pw_w', 'pw_b', 'bn2_g', 'bn2_b', 'bn2_m', 'bn2_v')}
    del _L1_conv_all

    def _L2_conv_setup():
        import math
        import jax, jax.numpy as jnp
        import numpy as np
        EPS_DIV = 1e-07
        EPS_NORM = 1e-12
        key = jax.random.key(seed)
        k1, k2, k3, k4, k5 = jax.random.split(key, 5)
        B, C, H, W = (8, 256, 32, 32)
        s = 1.0 / math.sqrt(C)
        return {'x': jax.random.normal(k1, (B, C, H, W), dtype=jnp.float32), 'Wqkv': jax.random.normal(k2, (C, 3 * C), dtype=jnp.float32) * s, 'bqkv': jax.random.normal(k3, (3 * C,), dtype=jnp.float32) * 0.01, 'Wln': jax.random.normal(k4, (C, C), dtype=jnp.float32) * s, 'bln': jax.random.normal(k5, (C,), dtype=jnp.float32) * 0.01}
    _L2_conv_all = _L2_conv_setup()
    _L2_conv_in = {k: v for k, v in _L2_conv_all.items() if k in ('Wqkv', 'bqkv', 'Wln', 'bln')}
    del _L2_conv_all

    def _L3_conv_setup():
        import jax, jax.numpy as jnp
        import numpy as np
        CHANNELS = [256, 128, 64, 32]
        key = jax.random.key(seed)
        x = jax.random.normal(key, (8, 256, 64, 64), dtype=jnp.float32)
        return {'x': x, 'ind': 0}
    _L3_conv_all = _L3_conv_setup()
    _L3_conv_in = {k: v for k, v in _L3_conv_all.items() if k in ()}
    del _L3_conv_all
    return {'x': x, 'L0_conv_gate_w': _L0_conv_in['gate_w'], 'L0_conv_gate_b': _L0_conv_in['gate_b'], 'L0_conv_expert_w': _L0_conv_in['expert_w'], 'L1_conv_dw_w': _L1_conv_in['dw_w'], 'L1_conv_dw_b': _L1_conv_in['dw_b'], 'L1_conv_bn1_g': _L1_conv_in['bn1_g'], 'L1_conv_bn1_b': _L1_conv_in['bn1_b'], 'L1_conv_bn1_m': _L1_conv_in['bn1_m'], 'L1_conv_bn1_v': _L1_conv_in['bn1_v'], 'L1_conv_pw_w': _L1_conv_in['pw_w'], 'L1_conv_pw_b': _L1_conv_in['pw_b'], 'L1_conv_bn2_g': _L1_conv_in['bn2_g'], 'L1_conv_bn2_b': _L1_conv_in['bn2_b'], 'L1_conv_bn2_m': _L1_conv_in['bn2_m'], 'L1_conv_bn2_v': _L1_conv_in['bn2_v'], 'L2_conv_Wqkv': _L2_conv_in['Wqkv'], 'L2_conv_bqkv': _L2_conv_in['bqkv'], 'L2_conv_Wln': _L2_conv_in['Wln'], 'L2_conv_bln': _L2_conv_in['bln']}

def reference(x, L0_conv_gate_w, L0_conv_gate_b, L0_conv_expert_w, L1_conv_dw_w, L1_conv_dw_b, L1_conv_bn1_g, L1_conv_bn1_b, L1_conv_bn1_m, L1_conv_bn1_v, L1_conv_pw_w, L1_conv_pw_b, L1_conv_bn2_g, L1_conv_bn2_b, L1_conv_bn2_m, L1_conv_bn2_v, L2_conv_Wqkv, L2_conv_bqkv, L2_conv_Wln, L2_conv_bln):
    import jax
    import jax.numpy as jnp

    def _L0_conv_ref(x, gate_w, gate_b, expert_w):
        import jax, jax.numpy as jnp
        import numpy as np
        STRIDE = 1

        def sparsemax(z):
            K = z.shape[-1]
            zs = -jnp.sort(-z, axis=-1)
            cum = jnp.cumsum(zs, axis=-1)
            ks = jnp.arange(1, K + 1, dtype=z.dtype)
            support = 1 + ks * zs > cum
            k_z = jnp.sum(support, axis=-1, keepdims=True)
            cum_k = jnp.take_along_axis(cum, k_z - 1, axis=-1)
            tau = (cum_k - 1) / k_z.astype(z.dtype)
            return jnp.maximum(z - tau, 0)
        pooled = x.mean(axis=(2, 3))
        g = sparsemax(pooled @ gate_w.T + gate_b)
        xs = x[:, :, ::STRIDE, ::STRIDE]
        w_eff = jnp.einsum('bk,koi->boi', g, expert_w)
        out = jnp.einsum('boi,bihw->bohw', w_eff, xs)
        return out

    def _L1_conv_ref(x, dw_w, dw_b, bn1_g, bn1_b, bn1_m, bn1_v, pw_w, pw_b, bn2_g, bn2_b, bn2_m, bn2_v):
        import jax, jax.numpy as jnp
        import numpy as np
        from jax import lax
        EPS = 1e-05
        DW_THRESH = 4.0
        PW_THRESH = 0.001
        C_IN = 256
        C_OUT = 256

        def _bn(x, g, b, m, v):
            inv = g * lax.rsqrt(v + EPS)
            return x * inv[None, :, None, None] + (b - m * inv)[None, :, None, None]

        def _prune(x, thresh):
            amax = jnp.max(jnp.abs(x), axis=(2, 3), keepdims=True)
            return jnp.where(amax < thresh, jnp.zeros_like(x), x)
        dn = ('NCHW', 'OIHW', 'NCHW')
        h = lax.conv_general_dilated(x, dw_w, window_strides=(1, 1), padding=((1, 1), (1, 1)), feature_group_count=C_IN, dimension_numbers=dn)
        h = h + dw_b[None, :, None, None]
        h = jax.nn.relu(_bn(h, bn1_g, bn1_b, bn1_m, bn1_v))
        h = _prune(h, DW_THRESH)
        h = lax.conv_general_dilated(h, pw_w, window_strides=(1, 1), padding=((0, 0), (0, 0)), dimension_numbers=dn)
        h = h + pw_b[None, :, None, None]
        h = jax.nn.relu(_bn(h, bn2_g, bn2_b, bn2_m, bn2_v))
        h = _prune(h, PW_THRESH)
        return h

    def _L2_conv_ref(x, Wqkv, bqkv, Wln, bln):
        import math
        import jax, jax.numpy as jnp
        import numpy as np
        EPS_DIV = 1e-07
        EPS_NORM = 1e-12
        B, C, H, W = x.shape
        N = H * W
        xt = x.reshape(B, C, N).transpose(0, 2, 1)
        qkv = xt @ Wqkv + bqkv
        q, k, v = jnp.split(qkv, 3, axis=2)
        q = q - jnp.mean(q, axis=2, keepdims=True)
        k = k - jnp.mean(k, axis=2, keepdims=True)
        q2 = q * q
        k2 = k * k
        q2s = jnp.sum(q2, axis=2, keepdims=True)
        k2s = jnp.sum(k2, axis=2, keepdims=True)
        k2n = k2 / (k2s + EPS_DIV)
        q2n = q2 / (q2s + EPS_DIV)
        k2n = k2n / jnp.maximum(jnp.linalg.norm(k2n, axis=-2, keepdims=True), EPS_NORM)
        q2n = q2n / jnp.maximum(jnp.linalg.norm(q2n, axis=-1, keepdims=True), EPS_NORM)
        kv = jnp.einsum('bnc,bnd->bcd', k2n, v)
        t2 = jnp.einsum('bnc,bcd->bnd', q2n, kv) / math.sqrt(N)
        attn = v + t2
        out = attn @ Wln + bln
        return out.reshape(B, H, W, C).transpose(0, 3, 1, 2)

    def _L3_conv_ref(x, ind):
        import jax, jax.numpy as jnp
        import numpy as np
        CHANNELS = [256, 128, 64, 32]
        C = CHANNELS[ind]
        assert x.shape[1] == C
        kernel = jnp.full((C, 1, 3, 3), 1.0 / 9.0, dtype=x.dtype)
        out = jax.lax.conv_general_dilated(x, kernel, window_strides=(1, 1), padding=((1, 1), (1, 1)), feature_group_count=C, dimension_numbers=('NCHW', 'OIHW', 'NCHW'))
        return out

    def _gn(v, G=32, eps=1e-05):
        B_, C_, H_, W_ = v.shape
        g = v.reshape(B_, G, C_ // G, H_, W_)
        m = jnp.mean(g, axis=(2, 3, 4), keepdims=True)
        s = jnp.var(g, axis=(2, 3, 4), keepdims=True)
        return ((g - m) / jnp.sqrt(s + eps)).reshape(v.shape)

    def _ln_c(v, eps=1e-06):
        m = jnp.mean(v, axis=1, keepdims=True)
        s = jnp.var(v, axis=1, keepdims=True)
        return (v - m) / jnp.sqrt(s + eps)

    def _ln_t(v, eps=1e-05):
        m = jnp.mean(v, axis=-1, keepdims=True)
        s = jnp.var(v, axis=-1, keepdims=True)
        return (v - m) / jnp.sqrt(s + eps)

    def _to_tokens(v):
        B_, C_, H_, W_ = v.shape
        return v.reshape(B_, C_, H_ * W_).transpose(0, 2, 1)

    def _from_tokens(t, like):
        B_, C_, H_, W_ = like.shape
        return t.transpose(0, 2, 1).reshape(B_, C_, H_, W_)
    x = x + _L0_conv_ref(_gn(x), L0_conv_gate_w, L0_conv_gate_b, L0_conv_expert_w)
    x = x + _L1_conv_ref(_gn(x), L1_conv_dw_w, L1_conv_dw_b, L1_conv_bn1_g, L1_conv_bn1_b, L1_conv_bn1_m, L1_conv_bn1_v, L1_conv_pw_w, L1_conv_pw_b, L1_conv_bn2_g, L1_conv_bn2_b, L1_conv_bn2_m, L1_conv_bn2_v)
    x = x + _L2_conv_ref(_gn(x), L2_conv_Wqkv, L2_conv_bqkv, L2_conv_Wln, L2_conv_bln)
    x = x + _L3_conv_ref(_gn(x), 0)
    return x

_drawn_inputs = setup_inputs


def setup_inputs(seed=0):
    import zlib

    import numpy as np

    out = dict(_drawn_inputs(seed))
    spreads = {'L1_conv_bn1_g': (1.0, 0.2),
     'L1_conv_bn1_b': (0.0, 0.1),
     'L1_conv_bn1_m': (0.0, 0.1),
     'L1_conv_bn1_v': (1.0, 0.2),
     'L1_conv_bn2_g': (1.0, 0.2),
     'L1_conv_bn2_b': (0.0, 0.1),
     'L1_conv_bn2_m': (0.0, 0.1),
     'L1_conv_bn2_v': (1.0, 0.2)}
    factors = {'L0_conv_gate_w': 6.791, 'L0_conv_gate_b': 4.358, 'L2_conv_bln': 6.685}
    for name, (base, spread) in spreads.items():
        noise = np.random.default_rng([zlib.crc32(name.encode()), seed]).standard_normal(out[name].shape)
        drawn = base * np.exp(spread * noise) if base else spread * noise
        out[name] = jnp.asarray(drawn.astype(out[name].dtype))
    for name, factor in factors.items():
        out[name] = (out[name] * factor).astype(out[name].dtype)
    return out
```

```python
from contextlib import ExitStack

import concourse.bass as bass
from concourse import mybir

ALU = mybir.AluOpType
ACT = mybir.ActivationFunctionType
F32 = mybir.dt.float32
BF16 = mybir.dt.bfloat16
AX = mybir.AxisListType

P = 128
IMAGES = 32
C = 256
J = C // P
H = W = 28
HW = H * W
HALF = HW // 2
CHUNKS = [(j, a) for j in range(J) for a in range(2)]
EXPERTS = 8
GROUP = C // 32
TAPS = 9
PH, PW = H + 2, W + 2
TOK = 112
M = HW // TOK
ROWS = TOK // W
BAND = (ROWS + 2) * W
UNROLL = 2
STAGES = 6
PARAMS = ["dw_b", "pw_b", "b_ln", "b_v", "bn1_g", "bn1_b", "bn1_m", "bn1_v", "bn2_g", "bn2_b", "bn2_m", "bn2_v"]

GN_EPS = 1e-5
BN_EPS = 1e-5
DW_THRESH = 4.0
PW_THRESH = 0.001
DIV_EPS = 1e-7
NORM_EPS = 1e-12

GN_STATS, GN_MV, GN_SQ, GN_SUMS, GN_VAR, GN_R, GN_DONE = 4, 6, 7, 9, 10, 11, 12


class Image:

    def __init__(self, pair, offset):
        self.pair, self.offset = pair, offset

    def __sub__(self, n):
        return Image(self.pair, self.offset - n)

    def __add__(self, n):
        return Image(self.pair, self.offset + n)

    def times(self, per, more=0):
        if self.pair is None:
            return per * self.offset + more
        return self.pair * (per * UNROLL) + (per * self.offset + more)

    @property
    def odd(self):
        return self.offset % 2

    @property
    def active(self):
        return self.pair is not None or 0 <= self.offset < IMAGES


class Count:

    def __init__(self, sem, per=1):
        self.sem, self.per = sem, per

    def at(self, image, count=None):
        return image.times(self.per, self.per if count is None else count)


class DmaCount:

    def __init__(self, sems):
        self.sems = sems

    def of(self, image):
        return self.sems[image.odd]

    def at(self, image):
        turn = 16 * (image.offset // 2 + 1)
        return turn if image.pair is None else image.pair * 16 + turn


def build(nc, x, gate_wT, gate_b, expert_wT, dw_w, channel_params, pw_wT, w_qk, b_qk, w_vT, w_ln, group_mean, ident,
          box_band, out):
    with ExitStack() as ctx:
        def sb(name, shape, dt=F32):
            return ctx.enter_context(nc.sbuf_tensor(name, shape, dt))

        def sem(name):
            return ctx.enter_context(nc.semaphore(name))

        def sig(name, per=1):
            return Count(sem(name), per)

        gate_w_sb = sb("gate_w_sb", [P, J, EXPERTS])
        gate_b_sb = sb("gate_b_sb", [P, EXPERTS])
        expert_sb = sb("expert_sb", [P, EXPERTS, J * C])
        dw_sb = sb("dw_sb", [P, J, TAPS])
        params = sb("params", [P, len(PARAMS), J])
        dwb_sb, pwb_sb, bln_sb, bv_col = (params[:, n, :] for n in range(4))
        bn1_sb, bn2_sb = params[:, 4:8, :], params[:, 8:12, :]
        pw_sb = sb("pw_sb", [P, J, C])
        wqk = sb("wqk", [P, J, 2 * C])
        wvT_sb = sb("wvT_sb", [P, J, C])
        wln_sb = sb("wln_sb", [P, J, C])
        bqk_row = sb("bqk_row", [1, 2 * C])
        gmean = sb("gmean", [P, P])
        idn = sb("idn", [P, P])
        box = sb("box", [TOK, BAND])
        ones = sb("ones", [P, P])
        ones3 = sb("ones3", [3, TOK], BF16)
        bqk_parts = sb("bqk_parts", [1, 3, 2 * C], BF16)
        bqk_rest = sb("bqk_rest", [1, 2, 2 * C])
        bqk3 = sb("bqk3", [3, 2 * C], BF16)
        bn_scale = sb("bn_scale", [P, 2, J])
        bn_shift = sb("bn_shift", [P, 2, J])
        bn_tmp = sb("bn_tmp", [P, 2, J])
        qk_mean = sb("qk_mean", [P, J, 2])
        bqk_mean = sb("bqk_mean", [1, 2])
        w_out = sb("w_out", [P, J, C])
        b_out = sb("b_out", [P, J])
        bv_ln = sb("bv_ln", [1, C])

        x0 = sb("x0", [P, 2, J, HW])
        xn0 = sb("xn0", [P, J, HW])
        mixed = sb("mixed", [P, 2, J * C])
        mix_tmp = sb("mix_tmp", [P, 2, J * C])
        x1 = sb("x1", [P, 2, J, HW])
        xpad = sb("xpad", [P, J, PH, PW])
        h = sb("h", [P, 2, J, HW])
        pw_masked = sb("pw_masked", [P, J, C])
        y = sb("y", [P, J, HW])
        x2 = sb("x2", [P, 2, J, HW])
        xn2 = sb("xn2", [P, 2, J, HW])
        q2 = sb("q2", [TOK, M, C])
        k2 = sb("k2", [TOK, M, C])
        q4 = sb("q4", [TOK, M, C], BF16)
        ksq = sb("ksq", [TOK, 2, C])
        ksum = sb("ksum", [TOK, 2, C])
        xT = sb("xT", [TOK, M, C])
        kx = sb("kx", [P, J, C])
        attn_w = sb("attn_w", [P, 2, J, C])
        qT = sb("qT", [P, J, HW])
        x3 = sb("x3", [P, 2, J, HW])
        xn3 = sb("xn3", [P, J, HW])
        x3T = sb("x3T", [TOK, M, C])

        bn6 = sb("bn6", [P, 4, 4, 6])
        gn_in = sb("gn_in", [P, 4, 6])
        gn_avg = sb("gn_avg", [P, 4, 6])
        gn_a = sb("gn_a", [P, 4, J])
        gn_b = sb("gn_b", [P, 4, J])
        gn_var = sb("gn_var", [P, 4, J])
        gn_sd = sb("gn_sd", [P, 4, J])
        gn_r = sb("gn_r", [P, 4, J])
        gn_s = sb("gn_s", [P, 4, J])
        pooled = sb("pooled", [P, 2, J])
        gate_in = sb("gate_in", [P, J, EXPERTS])
        z = sb("z", [P, EXPERTS])
        zz = sb("zz", [P, 2, EXPERTS, EXPERTS])
        excess = sb("excess", [P, EXPERTS])
        support = sb("support", [P, 2, EXPERTS])
        tau = sb("tau", [P, 4])
        gate = sb("gate", [P, EXPERTS])
        hmax = sb("hmax", [P, J])
        hmask = sb("hmask", [P, J])
        ymax = sb("ymax", [P, J])
        ymask = sb("ymask", [P, J])
        qk_sum = sb("qk_sum", [TOK, 2, M])
        qk_rec = sb("qk_rec", [TOK, 2, M])
        q_nsq = sb("q_nsq", [TOK, M])
        q_norm = sb("q_norm", [TOK, M])
        q_alpha = sb("q_alpha", [TOK, 3, M])
        k_norm = sb("k_norm", [P, C])
        k_inv = sb("k_inv", [P, 2, C])
        k_row = sb("k_row", [1, C])

        conv_ps = ctx.enter_context(nc.psum_tensor("conv_ps", [P, 4, 512], F32))
        tile_ps = ctx.enter_context(nc.psum_tensor("tile_ps", [P, 3, 512], F32))
        small_ps = ctx.enter_context(nc.psum_tensor("small_ps", [P, 512], F32))

        held = {name: sem(f"held_{name}") for name in ("dve", "pool", "sp")}

        def hold(eng, name):
            eng.sem_inc(held[name], 1)

        w_loaded = sem("w_loaded")
        setup_dve = sem("setup_dve")
        setup_act = sem("setup_act")
        setup_pe = sem("setup_pe")
        setup_pool = sem("setup_pool")
        bias_moved = sem("bias_moved")
        x_loaded = DmaCount([sem("x_loaded_even"), sem("x_loaded_odd")])
        stored = DmaCount([sem("stored_even"), sem("stored_odd")])
        gn = [sig(f"gn{n}", GN_DONE) for n in range(4)]
        gn_mm = [sig(f"gn_mm{n}") for n in range(4)]
        gn_read = [sig(f"gn_read{n}") for n in range(4)]
        gn_sqrt = [sig(f"gn_sqrt{n}") for n in range(4)]
        xn0_ready = sig("xn0_ready", J)
        gate_step = sig("gate_step", 14)
        gate_mm = sig("gate_mm")
        mix_step = sig("mix_step", 2 * EXPERTS - 1)
        conv0_mm = sig("conv0_mm", 4)
        x1_ready = sig("x1_ready", 4)
        xpad_ready = sig("xpad_ready", J)
        dw_step = sig("dw_step", J * TAPS)
        h_ready = sig("h_ready", J)
        hmask_step = sig("hmask_step", 2)
        pw_masked_ready = sig("pw_masked_ready", J)
        pw_mm = sig("pw_mm", 4)
        y_ready = sig("y_ready", 4)
        ymask_step = sig("ymask_step", 2)
        x2_ready = sig("x2_ready", J)
        xn2_ready = sig("xn2_ready", J)
        qk_mm = sig("qk_mm", M)
        q2_ready = sig("q2_ready", M)
        k2_ready = sig("k2_ready", M)
        rec_step = sig("rec_step", 2)
        kn_ready = sig("kn_ready", M)
        q4_ready = sig("q4_ready", M)
        q_root = sig("q_root")
        alpha_step = sig("alpha_step", 3)
        qa_ready = sig("qa_ready", M)
        ksum_step = sig("ksum_step", 3 * M - 2)
        xT_mm = sig("xT_mm", 4)
        xT_ready = sig("xT_ready", 4)
        kx_mm = sig("kx_mm")
        ksum_mm = sig("ksum_mm")
        k_root = sig("k_root")
        kinv_step = sig("kinv_step", 4)
        attn_w_mm = sig("attn_w_mm")
        attn_w_ready = sig("attn_w_ready")
        qT_mm = sig("qT_mm", 4)
        qT_ready = sig("qT_ready", 4)
        attn_mm = sig("attn_mm", 4)
        x3_ready = sig("x3_ready", 4)
        xn3_ready = sig("xn3_ready", J)
        x3T_mm = sig("x3T_mm", 4)
        x3T_ready = sig("x3T_ready", 4)
        box_mm = sig("box_mm", 4)
        x4_ready = sig("x4_ready", 4)

        x_dram = x.rearrange("b (j p) h w -> b p j (h w)", p=P)
        out_dram = out.rearrange("b (j p) h w -> b p j (h w)", p=P)

        def chunk(a):
            return slice(a * HALF, (a + 1) * HALF)

        def half(j):
            return slice(j * P, (j + 1) * P)

        def run(eng, step):
            first, last = 8, IMAGES
            for t in range(first):
                step(Image(None, t))
            with eng.Fori(first // UNROLL, last // UNROLL) as pair:
                for u in range(UNROLL):
                    step(Image(pair, u))
            for t in range(last, IMAGES + STAGES - 1):
                step(Image(None, t))

        PAIRS = [[2 * b, 2 * b + 1] if 2 * b + 1 < M else [2 * b] for b in range(4)]
        QUADS = [(j, ms) for j in range(J) for ms in ([0, 1, 2, 3], [4, 5, 6])]
        BOX = []
        for a in range(2):
            parts = []
            for m in range(M):
                lo, hi = max(m * TOK - W, a * HALF), min(m * TOK + TOK + W, (a + 1) * HALF)
                if lo < hi:
                    parts.append((m, lo - (m * TOK - W), lo - a * HALF, hi - lo))
            BOX.append(parts)

        block = ctx.enter_context(nc.Block())

        loads = [
            (gate_w_sb[:], gate_wT.rearrange("(j p) k -> p j k", p=P)),
            (gate_b_sb[:], gate_b[None, :].to_broadcast([P, EXPERTS])),
            (dw_sb[:], dw_w.rearrange("(j p) a b c -> p j (a b c)", p=P)),
            (params[:], channel_params),
            (bqk_row[:], b_qk[None, :]),
            (gmean[:], group_mean),
            (idn[:], ident),
            (box[:], box_band),
            (pw_sb[:], pw_wT.rearrange("(j p) o -> p j o", p=P)),
            (wqk[:], w_qk.rearrange("(j p) o -> p j o", p=P)),
            (wvT_sb[:], w_vT.rearrange("(j p) o -> p j o", p=P)),
            (wln_sb[:], w_ln.rearrange("(j p) o -> p j o", p=P)),
            *[(expert_sb[:, k, :].rearrange("p (j o) -> p j o", j=J),
               expert_wT[k].rearrange("(j p) o -> p j o", p=P)) for k in range(EXPERTS)],
        ]
        LOADED = 16 * len(loads)

        @block.sync
        def _(sp):
            def load(img):
                if img.active:
                    if (img - 2).active:
                        sp.wait_ge(x1_ready.sem, x1_ready.at(img - 2))
                    hold(sp, "sp")
                    sp.dma_start(x0[:, img.odd], x_dram[img.times(1)]).then_inc(x_loaded.of(img), 16)

            sp.dma_start(x0[:, 0], x_dram[0]).then_inc(x_loaded.sems[0], 16)
            for dst, src in loads:
                sp.dma_start(dst, src).then_inc(w_loaded, 16)

            def step(t):
                if t.pair is None and t.offset + 1 >= IMAGES:
                    pass
                else:
                    load(t - (-1))
                f = t - 5
                if f.active:
                    sp.wait_ge(x4_ready.sem, x4_ready.at(f))
                    sp.dma_start(out_dram[f.times(1)], x3[:, f.odd]).then_inc(stored.of(f), 16)

            first, last = 8, IMAGES
            for t in range(first):
                step(Image(None, t))
            with sp.Fori(first // UNROLL, last // UNROLL - 1) as pair:
                for u in range(UNROLL):
                    step(Image(pair, u))
            for t in range(last - UNROLL, IMAGES + STAGES - 1):
                step(Image(None, t))
            for last in (Image(None, IMAGES - 2), Image(None, IMAGES - 1)):
                sp.wait_ge(stored.of(last), stored.at(last))

        @block.tensor
        def _(pe):
            pe.wait_ge(w_loaded, LOADED)
            for i in range(J):
                for d in range(J):
                    mm = nc.tensor.matmul(conv_ps[:, i, 0:C], wvT_sb[:, d, half(i)], wln_sb[:, d, :],
                                          start=(d == 0), stop=(d == J - 1))
            mm.then_inc(setup_pe, 1)
            for o in range(J):
                for d in range(J):
                    mm = nc.tensor.matmul(conv_ps[:, 2, o:o + 1], wln_sb[:, d, half(o)], bv_col[:, d:d + 1],
                                          start=(d == 0), stop=(d == J - 1))
            for d in range(J):
                mm = nc.tensor.matmul(conv_ps[0:1, 3, 0:C], bv_col[:, d:d + 1], wln_sb[:, d, :],
                                      start=(d == 0), stop=(d == J - 1))
            mm.then_inc(setup_pe, 1)
            pe.wait_ge(setup_dve, SETUP_DVE)
            pe.wait_ge(setup_pool, 3)
            pe.wait_ge(bias_moved, 48)

            def wait_free(readers):
                for img, count, k in readers:
                    if img.active:
                        pe.wait_ge(count.sem, count.at(img, k))
                        return

            def group_means(layer, img):
                pe.wait_ge(gn[layer].sem, gn[layer].at(img, GN_SQ))
                nc.tensor.matmul(small_ps[:, 0:6], gmean[:], gn_in[:, layer, :], start=True,
                                 stop=True).then_inc(gn_mm[layer].sem, 1)

            def gate_logits(A):
                wait_free([(A, gn_read[0], 1)])
                pe.wait_ge(gate_step.sem, gate_step.at(A, 3))
                for j in range(J):
                    mm = nc.tensor.matmul(small_ps[:, 0:EXPERTS], ones[:], gate_in[:, j, :], start=(j == 0),
                                          stop=(j == J - 1))
                mm.then_inc(gate_mm.sem, 1)

            def conv_chunk(n, parts):
                j, a = CHUNKS[n]
                for i, (wt, act) in enumerate(parts):
                    mm = nc.tensor.matmul(conv_ps[:, n, 0:HALF], wt[:, half(j)], act[:, chunk(a)],
                                          start=(i == 0), stop=(i == len(parts) - 1))
                return mm

            def pointwise(C_):
                pe.wait_ge(h_ready.sem, h_ready.at(C_))
                pe.wait_ge(pw_masked_ready.sem, pw_masked_ready.at(C_))
                for n in range(4):
                    wait_free([(C_ - 4, x4_ready, n + 1), (C_ + 1, x1_ready, n + 1)])
                    conv_chunk(n, [(pw_masked[:, i, :], h[:, C_.odd, i, :]) for i in range(J)]
                               ).then_inc(pw_mm.sem, 1)

            def q_to_channels(E):
                pe.wait_ge(qa_ready.sem, qa_ready.at(E))
                before = [(E, attn_w_ready, 1), (E, kinv_step, 3), (E, kinv_step, 4), (E, qT_ready, 1)]
                for n, (j, ms) in enumerate(QUADS):
                    wait_free([before[n]])
                    for s, m in enumerate(ms):
                        mm = nc.tensor.transpose(tile_ps[:, QT_BANK[n], s * TOK:(s + 1) * TOK], q2[:, m, half(j)],
                                                 idn[0:TOK, 0:TOK])
                    mm.then_inc(qT_mm.sem, 1)

            def to_tokens(b, bank, source):
                for s, m in enumerate(PAIRS[b]):
                    for i in range(J):
                        mm = nc.tensor.transpose(tile_ps[0:TOK, bank, s * C + i * P:s * C + (i + 1) * P],
                                                 source[:, i, m * TOK:(m + 1) * TOK], idn[:])
                return mm

            def x3_to_tokens(F, E):
                pe.wait_ge(xn3_ready.sem, xn3_ready.at(F))
                before = [[(E, qT_ready, 2), (F - 1, x3T_ready, 4)], [(E, qT_ready, 3), (F - 1, x3T_ready, 2)],
                          [(E, qT_ready, 4), (F - 1, x3T_ready, 3)], [(F, x3T_ready, 1)]]
                for b in range(4):
                    wait_free(before[b])
                    to_tokens(b, X3T_BANK[b], xn3).then_inc(x3T_mm.sem, 1)

            def attention_out(E):
                pe.wait_ge(attn_w_ready.sem, attn_w_ready.at(E))
                pe.wait_ge(qT_ready.sem, qT_ready.at(E))
                for n in range(4):
                    wait_free([(E + 2, y_ready, n + 1), (E - 2, x4_ready, n + 1)])
                    conv_chunk(n, [(w_out[:, i, :], xn2[:, E.odd, i, :]) for i in range(J)]
                               + [(attn_w[:, E.odd, i, :], qT[:, i, :]) for i in range(J)]).then_inc(attn_mm.sem, 1)

            def queries_keys(D):
                pe.wait_ge(xn2_ready.sem, xn2_ready.at(D))
                before = [[(D - 2, x3T_ready, 2), (D - 1, qT_ready, 3)], [(D - 2, x3T_ready, 3), (D - 1, qT_ready, 4)],
                          [(D - 2, x3T_ready, 4), (D - 1, qT_ready, 2)]] + [[(D, k2_ready, m - 2)] for m in range(3, M)]
                for m in range(M):
                    wait_free(before[m])
                    bank = tile_ps[0:TOK, QK_BANK[m], :]
                    nc.tensor.matmul(bank, ones3[:], bqk3[:], start=True, stop=False)
                    for i in range(J):
                        mm = nc.tensor.matmul(bank, xn2[:, D.odd, i, m * TOK:(m + 1) * TOK], wqk[:, i, :],
                                              start=False, stop=(i == J - 1))
                    mm.then_inc(qk_mm.sem, 1)

            def x2_to_tokens(D):
                before = [(D, k2_ready, 5), (D, k2_ready, 6), (D, k2_ready, 7), (D, xT_ready, 1)]
                for b in range(4):
                    wait_free([before[b]])
                    to_tokens(b, XT_BANK[b], xn2[:, D.odd]).then_inc(xT_mm.sem, 1)

            def mixed_conv(A):
                pe.wait_ge(xn0_ready.sem, xn0_ready.at(A))
                pe.wait_ge(mix_step.sem, mix_step.at(A))
                for n in range(4):
                    wait_free([(A - 4, x3_ready, n + 1), (A - 2, y_ready, n + 1), (A - 1, x1_ready, n + 1)])
                    conv_chunk(n, [(mixed[:, A.odd, i * C:(i + 1) * C], xn0[:, i, :]) for i in range(J)]
                               ).then_inc(conv0_mm.sem, 1)

            def keys_x(D):
                pe.wait_ge(kn_ready.sem, kn_ready.at(D))
                pe.wait_ge(xT_ready.sem, xT_ready.at(D))
                for i in range(J):
                    for m in range(M):
                        mm = nc.tensor.matmul(tile_ps[:, KX_BANK, i * C:(i + 1) * C], xT[:, m, half(i)], k2[:, m, :],
                                              start=(m == 0), stop=(m == M - 1))
                mm.then_inc(kx_mm.sem, 1)
                pe.wait_ge(ksum_step.sem, ksum_step.at(D))
                nc.tensor.matmul(tile_ps[:, KSUM_BANK, :], ones[0:TOK, :], ksum[:], start=True,
                                 stop=True).then_inc(ksum_mm.sem, 1)

            def box_sums(F):
                pe.wait_ge(x3T_ready.sem, x3T_ready.at(F))
                for n, (j, a) in enumerate(CHUNKS):
                    wait_free([(F + 5, x1_ready, n + 1), (F + 1, x3_ready, n + 1), (F - 1, x4_ready, n + 1)])
                    for i, (m, src, dst, width) in enumerate(BOX[a]):
                        mm = nc.tensor.matmul(conv_ps[:, n, dst:dst + width], x3T[:, m, half(j)],
                                              box[:, src:src + width], start=(i == 0),
                                              stop=(i == len(BOX[a]) - 1), skip_group_check=True)
                    mm.then_inc(box_mm.sem, 1)

            def attention_weights(D):
                pe.wait_ge(kinv_step.sem, kinv_step.at(D))
                for c in range(J):
                    dst = tile_ps[:, ATTN_BANK, c * C:(c + 1) * C]
                    for i in range(J):
                        nc.tensor.matmul(dst, kx[:, i, half(c)], w_out[:, i, :], start=(i == 0), stop=False)
                    mm = nc.tensor.matmul(dst, k_row[:, half(c)], bv_ln[:], start=False, stop=True)
                mm.then_inc(attn_w_mm.sem, 1)

            def step(t):
                A, B, C_, D, E, F = (t - n for n in range(6))
                if A.active:
                    wait_free([(A - 1, gn_read[1], 1)])
                    group_means(0, A)
                if E.active:
                    q_to_channels(E)
                if C_.active:
                    pointwise(C_)
                if F.active:
                    x3_to_tokens(F, E)
                if A.active:
                    gate_logits(A)
                if E.active:
                    attention_out(E)
                if D.active:
                    queries_keys(D)
                if E.active:
                    wait_free([(A, gate_step, 4), (A - 1, gn_read[1], 1), (C_ - 1, gn_read[2], 1),
                               (E - 1, gn_read[3], 1)])
                    group_means(3, E)
                if C_.active:
                    wait_free([(E, gn_read[3], 1), (A, gate_step, 4)])
                    group_means(2, C_)
                if D.active:
                    x2_to_tokens(D)
                if A.active:
                    mixed_conv(A)
                if D.active:
                    keys_x(D)
                if F.active:
                    box_sums(F)
                if D.active:
                    attention_weights(D)
                if A.active:
                    wait_free([(C_, gn_read[2], 1), (E, gn_read[3], 1), (A, gate_step, 4)])
                    group_means(1, A)

            run(pe, step)

        @block.vector
        def _(dve):
            setup = [0]

            def did(ins):
                ins.then_inc(setup_dve, 1)
                setup[0] += 1
                dve.wait_ge(setup_dve, setup[0])

            dve.wait_ge(w_loaded, LOADED)
            for j in range(J):
                for s in range(2):
                    cols = slice(s * C, (s + 1) * C)
                    did(nc.vector.tensor_reduce(qk_mean[:, j, s:s + 1], wqk[:, j, cols], AX.X, ALU.add))
                    did(nc.vector.tensor_scalar(qk_mean[:, j, s:s + 1], qk_mean[:, j, s:s + 1], 1.0 / C, None, ALU.mult))
                    did(nc.vector.tensor_scalar(wqk[:, j, cols], wqk[:, j, cols], qk_mean[:, j, s:s + 1], None,
                                                ALU.subtract))
            for s in range(2):
                cols = slice(s * C, (s + 1) * C)
                did(nc.vector.tensor_reduce(bqk_mean[:, s:s + 1], bqk_row[:, cols], AX.X, ALU.add))
                did(nc.vector.tensor_scalar(bqk_mean[:, s:s + 1], bqk_mean[:, s:s + 1], 1.0 / C, None, ALU.mult))
                did(nc.vector.tensor_scalar(bqk_row[:, cols], bqk_row[:, cols], bqk_mean[:, s:s + 1], None,
                                            ALU.subtract))
            did(nc.vector.tensor_copy(bqk_parts[:, 0, :], bqk_row[:]))
            did(nc.vector.tensor_tensor(bqk_rest[:, 0, :], bqk_row[:], bqk_parts[:, 0, :], ALU.subtract))
            did(nc.vector.tensor_copy(bqk_parts[:, 1, :], bqk_rest[:, 0, :]))
            did(nc.vector.tensor_tensor(bqk_rest[:, 1, :], bqk_rest[:, 0, :], bqk_parts[:, 1, :], ALU.subtract))
            did(nc.vector.tensor_copy(bqk_parts[:, 2, :], bqk_rest[:, 1, :]))
            for n, (bn, bias) in enumerate(((bn1_sb, dwb_sb), (bn2_sb, pwb_sb))):
                did(nc.vector.tensor_scalar(bn_tmp[:, n, :], bn[:, 3, :], BN_EPS, None, ALU.add))
            dve.wait_ge(setup_act, 1)
            for n, (bn, bias) in enumerate(((bn1_sb, dwb_sb), (bn2_sb, pwb_sb))):
                did(nc.vector.reciprocal(bn_scale[:, n, :], bn_shift[:, n, :]))
                did(nc.vector.tensor_tensor(bn_scale[:, n, :], bn_scale[:, n, :], bn[:, 0, :], ALU.mult))
                did(nc.vector.tensor_tensor(bn_tmp[:, n, :], bias, bn[:, 2, :], ALU.subtract))
                did(nc.vector.tensor_tensor(bn_tmp[:, n, :], bn_tmp[:, n, :], bn_scale[:, n, :], ALU.mult))
                did(nc.vector.tensor_tensor(bn_shift[:, n, :], bn_tmp[:, n, :], bn[:, 1, :], ALU.add))
            dve.wait_ge(setup_pe, 2)
            did(nc.vector.tensor_copy(w_out[:], conv_ps[:, 0:2, 0:C]))
            did(nc.vector.tensor_tensor(b_out[:], conv_ps[:, 2, 0:J], bln_sb, ALU.add))
            did(nc.vector.tensor_copy(bv_ln[:], conv_ps[0:1, 3, 0:C]))
            assert setup[0] == SETUP_DVE

            def statistics(layer, img, source, ready):
                s = gn[layer]
                for q, (j, a) in enumerate(CHUNKS):
                    if ready is not None and q * ready.per % 4 == 0:
                        dve.wait_ge(ready.sem, ready.at(img, q * ready.per // 4 + 1))
                    nc.vector.bn_stats(bn6[:, layer, q, :], source[:, j, chunk(a)]).then_inc(s.sem, 1)
                dve.wait_ge(s.sem, s.at(img, GN_STATS))
                if (img - 1).active:
                    dve.wait_ge(gn_mm[layer].sem, gn_mm[layer].at(img - 1))
                hold(dve, "dve")
                for j in range(J):
                    nc.vector.bn_aggr(gn_in[:, layer, 2 * j:2 * j + 2],
                                      bn6[:, layer, 2 * j:2 * j + 2, :]).then_inc(s.sem, 1)
                dve.wait_ge(s.sem, s.at(img, GN_MV))
                nc.vector.tensor_tensor(gn_in[:, layer, 4:6], gn_in[:, layer, 0:4:2], gn_in[:, layer, 0:4:2],
                                        ALU.mult).then_inc(s.sem, 1)

            def variance(layer, img):
                s = gn[layer]
                dve.wait_ge(gn_mm[layer].sem, gn_mm[layer].at(img))
                nc.vector.tensor_copy(gn_avg[:, layer, :], small_ps[:, 0:6]).then_inc(gn_read[layer].sem, 1)
                dve.wait_ge(gn_read[layer].sem, gn_read[layer].at(img))
                mean, var, sq = gn_avg[:, layer, 0:4:2], gn_avg[:, layer, 1:4:2], gn_avg[:, layer, 4:6]
                nc.vector.scalar_tensor_tensor(gn_a[:, layer, :], var, GN_EPS, sq, ALU.add, ALU.add).then_inc(s.sem, 1)
                nc.vector.tensor_tensor(gn_b[:, layer, :], mean, mean, ALU.mult).then_inc(s.sem, 1)
                dve.wait_ge(s.sem, s.at(img, GN_SUMS))
                nc.vector.tensor_tensor(gn_var[:, layer, :], gn_a[:, layer, :], gn_b[:, layer, :],
                                        ALU.subtract).then_inc(s.sem, 1)

            def scale_shift(layer, img):
                s = gn[layer]
                dve.wait_ge(gn_sqrt[layer].sem, gn_sqrt[layer].at(img))
                nc.vector.reciprocal(gn_r[:, layer, :], gn_sd[:, layer, :]).then_inc(s.sem, 1)
                dve.wait_ge(s.sem, s.at(img, GN_R))
                nc.vector.scalar_tensor_tensor(gn_s[:, layer, :], gn_avg[:, layer, 0:4:2], -1.0, gn_r[:, layer, :],
                                               ALU.mult, ALU.mult).then_inc(s.sem, 1)

            def gate_logits(A):
                s = gate_step
                dve.wait_ge(gn[0].sem, gn[0].at(A))
                nc.vector.tensor_tensor(pooled[:, 0, :], gn_in[:, 0, 0:4:2], gn_r[:, 0, :], ALU.mult).then_inc(s.sem, 1)
                dve.wait_ge(s.sem, s.at(A, 1))
                nc.vector.tensor_tensor(pooled[:, 1, :], pooled[:, 0, :], gn_s[:, 0, :], ALU.add).then_inc(s.sem, 1)
                dve.wait_ge(s.sem, s.at(A, 2))
                if (A - 1).active:
                    dve.wait_ge(gate_mm.sem, gate_mm.at(A - 1))
                nc.vector.tensor_tensor(gate_in[:], gate_w_sb[:],
                                        pooled[:, 1, :].unsqueeze(2).to_broadcast([P, J, EXPERTS]),
                                        ALU.mult).then_inc(s.sem, 1)

            def sparsemax(A):
                s = gate_step
                dve.wait_ge(gate_mm.sem, gate_mm.at(A))
                nc.vector.tensor_tensor(z[:], small_ps[:, 0:EXPERTS], gate_b_sb[:], ALU.add).then_inc(s.sem, 1)
                dve.wait_ge(s.sem, s.at(A, 4))
                nc.vector.tensor_tensor(zz[:, 0], z[:].unsqueeze(1).to_broadcast([P, EXPERTS, EXPERTS]),
                                        z[:].unsqueeze(2).to_broadcast([P, EXPERTS, EXPERTS]),
                                        ALU.subtract).then_inc(s.sem, 1)
                dve.wait_ge(s.sem, s.at(A, 5))
                nc.vector.tensor_scalar(zz[:, 1], zz[:, 0], 0.0, None, ALU.max).then_inc(s.sem, 1)
                dve.wait_ge(s.sem, s.at(A, 6))
                nc.vector.tensor_reduce(excess[:], zz[:, 1], AX.X, ALU.add).then_inc(s.sem, 1)
                dve.wait_ge(s.sem, s.at(A, 7))
                nc.vector.tensor_scalar(support[:, 0, :], excess[:], 1.0, None, ALU.is_lt).then_inc(s.sem, 1)
                dve.wait_ge(s.sem, s.at(A, 8))
                nc.vector.tensor_tensor(support[:, 1, :], support[:, 0, :], z[:], ALU.mult).then_inc(s.sem, 1)
                dve.wait_ge(s.sem, s.at(A, 9))
                nc.vector.tensor_reduce(tau[:, 0:2], support[:], AX.X, ALU.add).then_inc(s.sem, 1)
                dve.wait_ge(s.sem, s.at(A, 10))
                nc.vector.reciprocal(tau[:, 2:3], tau[:, 0:1]).then_inc(s.sem, 1)
                nc.vector.tensor_scalar(tau[:, 1:2], tau[:, 1:2], -1.0, None, ALU.add).then_inc(s.sem, 1)
                dve.wait_ge(s.sem, s.at(A, 12))
                nc.vector.tensor_tensor(tau[:, 3:4], tau[:, 1:2], tau[:, 2:3], ALU.mult).then_inc(s.sem, 1)
                dve.wait_ge(s.sem, s.at(A, 13))
                if (A - 1).active:
                    dve.wait_ge(mix_step.sem, mix_step.at(A - 1))
                nc.vector.tensor_scalar(gate[:], z[:], tau[:, 3:4], 0.0, ALU.subtract, ALU.max).then_inc(s.sem, 1)

            def depthwise(B, j):
                dve.wait_ge(xpad_ready.sem, xpad_ready.at(B, j + 1))
                if (B - 2).active:
                    dve.wait_ge(pw_mm.sem, pw_mm.at(B - 2))
                acc = h[:, B.odd, j, :].rearrange("p (h w) -> p h w", w=W)
                for tap in range(TAPS):
                    view = xpad[:, j, tap // 3:tap // 3 + H, tap % 3:tap % 3 + W]
                    scalar = dw_sb[:, j, tap:tap + 1]
                    if tap == 0:
                        ins = nc.vector.tensor_scalar(acc, view, scalar, None, ALU.mult)
                    else:
                        dve.wait_ge(dw_step.sem, dw_step.at(B, j * TAPS + tap))
                        ins = nc.vector.scalar_tensor_tensor(acc, view, scalar, acc, ALU.mult, ALU.add)
                    ins.then_inc(dw_step.sem, 1)

            def h_mask(B):
                dve.wait_ge(h_ready.sem, h_ready.at(B))
                nc.vector.tensor_reduce(hmax[:], h[:, B.odd], AX.X, ALU.max).then_inc(hmask_step.sem, 1)
                dve.wait_ge(hmask_step.sem, hmask_step.at(B, 1))
                if (B - 1).active:
                    dve.wait_ge(pw_masked_ready.sem, pw_masked_ready.at(B - 1))
                nc.vector.tensor_scalar(hmask[:], hmax[:], DW_THRESH, None, ALU.is_ge).then_inc(hmask_step.sem, 1)

            def make_x2(C_):
                dve.wait_ge(y_ready.sem, y_ready.at(C_))
                nc.vector.tensor_reduce(ymax[:], y[:], AX.X, ALU.max).then_inc(ymask_step.sem, 1)
                dve.wait_ge(ymask_step.sem, ymask_step.at(C_, 1))
                nc.vector.tensor_scalar(ymask[:], ymax[:], PW_THRESH, None, ALU.is_ge).then_inc(ymask_step.sem, 1)
                dve.wait_ge(ymask_step.sem, ymask_step.at(C_, 2))
                if (C_ - 2).active:
                    dve.wait_ge(x3_ready.sem, x3_ready.at(C_ - 2))
                for j in range(J):
                    nc.vector.scalar_tensor_tensor(x2[:, C_.odd, j, :], y[:, j, :], ymask[:, j:j + 1],
                                                   x1[:, C_.odd, j, :], ALU.mult, ALU.add).then_inc(x2_ready.sem, 1)

            def add_conv0(A):
                if (A - 2).active:
                    dve.wait_ge(x2_ready.sem, x2_ready.at(A - 2))
                if (A - 2).active:
                    dve.wait_ge(xpad_ready.sem, xpad_ready.at(A - 2))
                for n, (j, a) in enumerate(CHUNKS):
                    dve.wait_ge(conv0_mm.sem, conv0_mm.at(A, n + 1))
                    nc.vector.tensor_tensor(x1[:, A.odd, j, chunk(a)], conv_ps[:, n, 0:HALF],
                                            x0[:, A.odd, j, chunk(a)], ALU.add).then_inc(x1_ready.sem, 1)

            def make_x3(E):
                if (E - 2).active:
                    dve.wait_ge(stored.of(E - 2), stored.at(E - 2))
                for n, (j, a) in enumerate(CHUNKS):
                    dve.wait_ge(attn_mm.sem, attn_mm.at(E, n + 1))
                    nc.vector.scalar_tensor_tensor(x3[:, E.odd, j, chunk(a)], conv_ps[:, n, 0:HALF], b_out[:, j:j + 1],
                                                   x2[:, E.odd, j, chunk(a)], ALU.add,
                                                   ALU.add).then_inc(x3_ready.sem, 1)

            def make_x4(F):
                for n, (j, a) in enumerate(CHUNKS):
                    dve.wait_ge(box_mm.sem, box_mm.at(F, n + 1))
                    nc.vector.scalar_tensor_tensor(x3[:, F.odd, j, chunk(a)], conv_ps[:, n, 0:HALF], 1.0 / TAPS,
                                                   x3[:, F.odd, j, chunk(a)], ALU.mult,
                                                   ALU.add).then_inc(x4_ready.sem, 1)

            def normalise_k(D):
                dve.wait_ge(q2_ready.sem, q2_ready.at(D))
                dve.wait_ge(k2_ready.sem, k2_ready.at(D))
                nc.vector.tensor_scalar(qk_rec[:], qk_sum[:], DIV_EPS, None, ALU.add).then_inc(rec_step.sem, 1)
                dve.wait_ge(rec_step.sem, rec_step.at(D, 1))
                nc.vector.reciprocal(qk_rec[:], qk_rec[:]).then_inc(rec_step.sem, 1)
                dve.wait_ge(rec_step.sem, rec_step.at(D, 2))
                for m in range(M):
                    nc.vector.tensor_scalar(k2[:, m, :], k2[:, m, :], qk_rec[:, 1, m:m + 1], None,
                                            ALU.mult).then_inc(kn_ready.sem, 1)

            def scale_q(D):
                dve.wait_ge(q_root.sem, q_root.at(D))
                nc.vector.tensor_scalar(q_alpha[:, 0, :], q_norm[:], NORM_EPS, None, ALU.max).then_inc(alpha_step.sem, 1)
                dve.wait_ge(alpha_step.sem, alpha_step.at(D, 1))
                nc.vector.reciprocal(q_alpha[:, 1, :], q_alpha[:, 0, :]).then_inc(alpha_step.sem, 1)
                dve.wait_ge(alpha_step.sem, alpha_step.at(D, 2))
                nc.vector.scalar_tensor_tensor(q_alpha[:, 2, :], q_alpha[:, 1, :], float(HW) ** -0.5, qk_rec[:, 0, :],
                                               ALU.mult, ALU.mult).then_inc(alpha_step.sem, 1)
                dve.wait_ge(alpha_step.sem, alpha_step.at(D, 3))
                for m in range(M):
                    nc.vector.tensor_scalar(q2[:, m, :], q2[:, m, :], q_alpha[:, 2, m:m + 1], None,
                                            ALU.mult).then_inc(qa_ready.sem, 1)

            def scale_kx(D):
                dve.wait_ge(k_root.sem, k_root.at(D))
                nc.vector.tensor_scalar(k_inv[:, 0, :], k_norm[:], NORM_EPS, None, ALU.max).then_inc(kinv_step.sem, 1)
                dve.wait_ge(kinv_step.sem, kinv_step.at(D, 1))
                nc.vector.reciprocal(k_inv[:, 1, :], k_inv[:, 0, :]).then_inc(kinv_step.sem, 1)
                dve.wait_ge(kinv_step.sem, kinv_step.at(D, 2))
                dve.wait_ge(kx_mm.sem, kx_mm.at(D))
                if (D - 1).active:
                    dve.wait_ge(attn_w_mm.sem, attn_w_mm.at(D - 1))
                nc.vector.tensor_tensor(kx[:], tile_ps[:, KX_BANK, :].rearrange("p (i c) -> p i c", i=J),
                                        k_inv[:, 1, :].unsqueeze(1).to_broadcast([P, J, C]),
                                        ALU.mult).then_inc(kinv_step.sem, 1)
                nc.vector.tensor_tensor(k_row[:], tile_ps[0:1, KSUM_BANK, 0:C], k_inv[0:1, 1, :],
                                        ALU.mult).then_inc(kinv_step.sem, 1)

            def step(t):
                A, B, C_, D, E, F = (t - n for n in range(6))
                if A.active:
                    dve.wait_ge(x_loaded.of(A), x_loaded.at(A))
                    statistics(0, A, x0[:, A.odd], None)
                    variance(0, A)
                    scale_shift(0, A)
                    gate_logits(A)
                if E.active:
                    make_x3(E)
                    statistics(3, E, x3[:, E.odd], x3_ready)
                if A.active:
                    sparsemax(A)
                if C_.active:
                    make_x2(C_)
                    statistics(2, C_, x2[:, C_.odd], x2_ready)
                if B.active:
                    depthwise(B, 0)
                if E.active:
                    variance(3, E)
                    scale_shift(3, E)
                if C_.active:
                    variance(2, C_)
                    scale_shift(2, C_)
                if D.active:
                    normalise_k(D)
                    scale_q(D)
                if B.active:
                    depthwise(B, 1)
                if A.active:
                    add_conv0(A)
                    statistics(1, A, x1[:, A.odd], x1_ready)
                if D.active:
                    scale_kx(D)
                if B.active:
                    h_mask(B)
                if F.active:
                    make_x4(F)
                if A.active:
                    variance(1, A)
                    scale_shift(1, A)

            run(dve, step)

        @block.scalar
        def _(act):
            act.wait_ge(setup_dve, SETUP_BN)
            nc.scalar.activation(bn_shift[:], bn_tmp[:], ACT.Sqrt).then_inc(setup_act, 1)
            for k in range(3):
                act.dma_start(bqk3[k:k + 1, :], bqk_parts[:, k, :]).then_inc(bias_moved, 16)
            act.wait_ge(setup_dve, SETUP_DVE)

            def deviation(layer, img):
                act.wait_ge(gn[layer].sem, gn[layer].at(img, GN_VAR))
                nc.scalar.activation(gn_sd[:, layer, :], gn_var[:, layer, :], ACT.Sqrt).then_inc(gn_sqrt[layer].sem, 1)

            def normalise(layer, img, outs, source, signal):
                act.wait_ge(gn[layer].sem, gn[layer].at(img))
                for j in range(J):
                    nc.scalar.activation(outs[j], source[j], ACT.Identity, bias=gn_s[:, layer, j:j + 1],
                                         scale=gn_r[:, layer, j:j + 1]).then_inc(signal.sem, 1)

            def copy_tiles(img, banks, mm, ready, dst):
                for b, ms in enumerate(PAIRS):
                    act.wait_ge(mm.sem, mm.at(img, b + 1))
                    bank = banks[b]
                    nc.scalar.copy(dst[:, ms[0]:ms[-1] + 1, :],
                                   tile_ps[0:TOK, bank, 0:len(ms) * C].rearrange("p (m c) -> p m c", c=C)
                                   ).then_inc(ready.sem, 1)

            def step(t):
                A, B, C_, D, E, F = (t - n for n in range(6))
                if A.active:
                    deviation(0, A)
                if E.active:
                    if (E - 1).active:
                        act.wait_ge(attn_mm.sem, attn_mm.at(E - 1))
                    for n, (j, ms) in enumerate(QUADS):
                        act.wait_ge(qT_mm.sem, qT_mm.at(E, n + 1))
                        nc.scalar.copy(qT[:, j, ms[0] * TOK:(ms[-1] + 1) * TOK],
                                       tile_ps[:, QT_BANK[n], 0:len(ms) * TOK]).then_inc(qT_ready.sem, 1)
                if C_.active:
                    if (C_ - 1).active:
                        act.wait_ge(x2_ready.sem, x2_ready.at(C_ - 1))
                    for n, (j, a) in enumerate(CHUNKS):
                        act.wait_ge(pw_mm.sem, pw_mm.at(C_, n + 1))
                        nc.scalar.activation(y[:, j, chunk(a)], conv_ps[:, n, 0:HALF], ACT.Relu,
                                             bias=bn_shift[:, 1, j:j + 1],
                                             scale=bn_scale[:, 1, j:j + 1]).then_inc(y_ready.sem, 1)
                if A.active:
                    if (A - 1).active:
                        act.wait_ge(conv0_mm.sem, conv0_mm.at(A - 1))
                    normalise(0, A, [xn0[:, j, :] for j in range(J)], [x0[:, A.odd, j, :] for j in range(J)],
                              xn0_ready)
                if F.active:
                    if (F - 1).active:
                        act.wait_ge(box_mm.sem, box_mm.at(F - 1))
                    copy_tiles(F, X3T_BANK, x3T_mm, x3T_ready, x3T)
                if D.active:
                    if (D - 1).active:
                        act.wait_ge(qT_mm.sem, qT_mm.at(D - 1))
                    if (D - 1).active:
                        act.wait_ge(kx_mm.sem, kx_mm.at(D - 1))
                    if (D - 1).active:
                        act.wait_ge(ksum_step.sem, ksum_step.at(D - 1))
                    if (D - 1).active:
                        act.wait_ge(rec_step.sem, rec_step.at(D - 1))
                    for m in range(M):
                        act.wait_ge(qk_mm.sem, qk_mm.at(D, m + 1))
                        bank = tile_ps[0:TOK, QK_BANK[m], :]
                        nc.scalar.activation(q2[:, m, :], bank[:, 0:C], ACT.Square,
                                             accum_out=qk_sum[:, 0, m:m + 1]).then_inc(q2_ready.sem, 1)
                        nc.scalar.activation(k2[:, m, :], bank[:, C:2 * C], ACT.Square,
                                             accum_out=qk_sum[:, 1, m:m + 1]).then_inc(k2_ready.sem, 1)
                if E.active:
                    deviation(3, E)
                if C_.active:
                    deviation(2, C_)
                if E.active:
                    if (E - 1).active:
                        act.wait_ge(x3T_mm.sem, x3T_mm.at(E - 1))
                    normalise(3, E, [xn3[:, j, :] for j in range(J)], [x3[:, E.odd, j, :] for j in range(J)],
                              xn3_ready)
                if C_.active:
                    if (C_ - 2).active:
                        act.wait_ge(attn_mm.sem, attn_mm.at(C_ - 2))
                    normalise(2, C_, [xn2[:, C_.odd, j, :] for j in range(J)],
                              [x2[:, C_.odd, j, :] for j in range(J)], xn2_ready)
                if D.active:
                    if (D - 1).active:
                        act.wait_ge(kx_mm.sem, kx_mm.at(D - 1))
                    copy_tiles(D, XT_BANK, xT_mm, xT_ready, xT)
                if D.active:
                    act.wait_ge(rec_step.sem, rec_step.at(D))
                    for m in range(M):
                        nc.scalar.activation(q4[:, m, :], q2[:, m, :], ACT.Square, scale=qk_rec[:, 0, m:m + 1],
                                             accum_out=q_nsq[:, m:m + 1]).then_inc(q4_ready.sem, 1)
                    act.wait_ge(q4_ready.sem, q4_ready.at(D))
                    nc.scalar.activation(q_norm[:], q_nsq[:], ACT.Sqrt).then_inc(q_root.sem, 1)
                if B.active:
                    act.wait_ge(dw_step.sem, dw_step.at(B, TAPS))
                    nc.scalar.activation(h[:, B.odd, 0, :], h[:, B.odd, 0, :], ACT.Relu, bias=bn_shift[:, 0, 0:1],
                                         scale=bn_scale[:, 0, 0:1]).then_inc(h_ready.sem, 1)
                if D.active:
                    act.wait_ge(ksum_mm.sem, ksum_mm.at(D))
                    nc.scalar.activation(k_norm[:], tile_ps[:, KSUM_BANK, C:2 * C], ACT.Sqrt).then_inc(k_root.sem, 1)
                if B.active:
                    act.wait_ge(dw_step.sem, dw_step.at(B))
                    nc.scalar.activation(h[:, B.odd, 1, :], h[:, B.odd, 1, :], ACT.Relu, bias=bn_shift[:, 0, 1:2],
                                         scale=bn_scale[:, 0, 1:2]).then_inc(h_ready.sem, 1)
                if D.active:
                    if (D - 2).active:
                        act.wait_ge(attn_mm.sem, attn_mm.at(D - 2))
                    act.wait_ge(attn_w_mm.sem, attn_w_mm.at(D))
                    nc.scalar.copy(attn_w[:, D.odd], tile_ps[:, ATTN_BANK, :].rearrange("p (c o) -> p c o", c=J)
                                   ).then_inc(attn_w_ready.sem, 1)
                if A.active:
                    deviation(1, A)
                    if (A - 1).active:
                        act.wait_ge(dw_step.sem, dw_step.at(A - 1))
                    act.wait_ge(setup_pool, 3)
                    normalise(1, A, [xpad[:, j, 1:1 + H, 1:1 + W] for j in range(J)],
                              [x1[:, A.odd, j, :].rearrange("p (h w) -> p h w", w=W) for j in range(J)], xpad_ready)

            run(act, step)

        @block.gpsimd
        def _(pool):
            nc.gpsimd.memset(ones[:], 1.0).then_inc(setup_pool, 1)
            nc.gpsimd.memset(ones3[:], 1.0).then_inc(setup_pool, 1)
            nc.gpsimd.memset(xpad[:], 0.0).then_inc(setup_pool, 1)

            def mask_weights(B):
                if (B - 1).active:
                    pool.wait_ge(pw_mm.sem, pw_mm.at(B - 1))
                pool.wait_ge(hmask_step.sem, hmask_step.at(B))
                hold(pool, "pool")
                for j in range(J):
                    nc.gpsimd.tensor_scalar(pw_masked[:, j, :], pw_sb[:, j, :], hmask[:, j:j + 1], 0.0, ALU.mult,
                                            ALU.add).then_inc(pw_masked_ready.sem, 1)

            def mix(A):
                if (A - 2).active:
                    pool.wait_ge(conv0_mm.sem, conv0_mm.at(A - 2))
                pool.wait_ge(gate_step.sem, gate_step.at(A))
                hold(pool, "pool")
                done = 0
                for k in range(EXPERTS):
                    dst = mixed[:, A.odd, :] if k == 0 else mix_tmp[:, k % 2, :]
                    if k >= 3:
                        pool.wait_ge(mix_step.sem, mix_step.at(A, 2 * (k - 2) + 1))
                        hold(pool, "pool")
                    nc.gpsimd.tensor_scalar(dst, expert_sb[:, k, :], gate[:, k:k + 1], 0.0, ALU.mult,
                                            ALU.add).then_inc(mix_step.sem, 1)
                    done += 1
                    if k:
                        pool.wait_ge(mix_step.sem, mix_step.at(A, done))
                        nc.gpsimd.tensor_tensor(mixed[:, A.odd, :], mixed[:, A.odd, :], mix_tmp[:, k % 2, :],
                                                ALU.add).then_inc(mix_step.sem, 1)
                        done += 1

            def sum_k(D):
                if (D - 1).active:
                    pool.wait_ge(ksum_mm.sem, ksum_mm.at(D - 1))
                done = 0
                for m in range(M):
                    pool.wait_ge(kn_ready.sem, kn_ready.at(D, m + 1))
                    if m == 0:
                        nc.gpsimd.tensor_tensor(ksum[:, 1, :], k2[:, 0, :], k2[:, 0, :], ALU.mult).then_inc(
                            ksum_step.sem, 1)
                        done += 1
                        continue
                    if m >= 3:
                        pool.wait_ge(ksum_step.sem, ksum_step.at(D, 3 * (m - 2) + 1))
                    nc.gpsimd.tensor_tensor(ksq[:, m % 2, :], k2[:, m, :], k2[:, m, :], ALU.mult).then_inc(
                        ksum_step.sem, 1)
                    a = k2[:, 0, :] if m == 1 else ksum[:, 0, :]
                    nc.gpsimd.tensor_tensor(ksum[:, 0, :], a, k2[:, m, :], ALU.add).then_inc(ksum_step.sem, 1)
                    done += 2
                    pool.wait_ge(ksum_step.sem, ksum_step.at(D, done))
                    nc.gpsimd.tensor_tensor(ksum[:, 1, :], ksum[:, 1, :], ksq[:, m % 2, :], ALU.add).then_inc(
                        ksum_step.sem, 1)
                    done += 1

            def step(t):
                A, B, C_, D, E, F = (t - n for n in range(6))
                if A.active:
                    mix(A)
                if D.active:
                    sum_k(D)
                if B.active:
                    mask_weights(B)

            run(pool, step)


SETUP_PARTS = 12 + 6 + 5
SETUP_BN = SETUP_PARTS + 2
SETUP_DVE = SETUP_BN + 10 + 3
BANKS = [n % 3 for n in range(4 + 4 + M + 4 + 3)]
QT_BANK, X3T_BANK, QK_BANK, XT_BANK = BANKS[0:4], BANKS[4:8], BANKS[8:8 + M], BANKS[8 + M:12 + M]
KX_BANK, KSUM_BANK, ATTN_BANK = BANKS[12 + M:]


def kernel(x, L0_conv_gate_w, L0_conv_gate_b, L0_conv_expert_w, L1_conv_dw_w, L1_conv_dw_b, L1_conv_bn1_g,
           L1_conv_bn1_b, L1_conv_bn1_m, L1_conv_bn1_v, L1_conv_pw_w, L1_conv_pw_b, L1_conv_bn2_g, L1_conv_bn2_b,
           L1_conv_bn2_m, L1_conv_bn2_v, L2_conv_Wqkv, L2_conv_bqkv, L2_conv_Wln, L2_conv_bln):
    import numpy as np
    import concourse.bacc as bacc
    from concourse.bass_utils import run_bass_kernel_spmd

    c = np.arange(P)
    group_mean = ((c[:, None] // GROUP) == (c[None, :] // GROUP)).astype(np.float32) / GROUP
    tok, col = np.arange(TOK), np.arange(BAND)
    near_row = np.abs(tok[:, None] // W + 1 - col[None, :] // W) <= 1
    near_col = np.abs(tok[:, None] % W - col[None, :] % W) <= 1
    per_channel = {
        "dw_b": L1_conv_dw_b, "pw_b": L1_conv_pw_b, "b_ln": L2_conv_bln, "b_v": np.asarray(L2_conv_bqkv)[2 * C:],
        "bn1_g": L1_conv_bn1_g, "bn1_b": L1_conv_bn1_b, "bn1_m": L1_conv_bn1_m, "bn1_v": L1_conv_bn1_v,
        "bn2_g": L1_conv_bn2_g, "bn2_b": L1_conv_bn2_b, "bn2_m": L1_conv_bn2_m, "bn2_v": L1_conv_bn2_v,
    }
    arrays = {
        "x": x,
        "gate_wT": np.asarray(L0_conv_gate_w).T,
        "gate_b": L0_conv_gate_b,
        "expert_wT": np.asarray(L0_conv_expert_w).transpose(0, 2, 1),
        "dw_w": L1_conv_dw_w,
        "channel_params": np.stack([np.asarray(per_channel[name]).reshape(J, P) for name in PARAMS]).transpose(2, 0, 1),
        "pw_wT": np.asarray(L1_conv_pw_w)[:, :, 0, 0].T,
        "w_qk": np.asarray(L2_conv_Wqkv)[:, :2 * C],
        "b_qk": np.asarray(L2_conv_bqkv)[:2 * C],
        "w_vT": np.asarray(L2_conv_Wqkv)[:, 2 * C:].T,
        "w_ln": L2_conv_Wln,
        "group_mean": group_mean,
        "ident": np.eye(P, dtype=np.float32),
        "box_band": (near_row & near_col).astype(np.float32),
    }
    arrays = {name: np.ascontiguousarray(a) for name, a in arrays.items()}
    nc = bacc.Bacc("TRN2", target_bir_lowering=False, num_devices=1)
    t = {name: nc.dram_tensor(name, a.shape, mybir.dt.from_np(a.dtype), kind="ExternalInput").ap()
         for name, a in arrays.items()}
    out = nc.dram_tensor("out", (IMAGES, C, H, W), F32, kind="ExternalOutput").ap()
    build(nc, out=out, **t)
    r = run_bass_kernel_spmd(nc, [arrays], core_ids=[0])
    return r.results[0]["out"]
```

```python
from contextlib import ExitStack

import concourse.bass as bass
from concourse import mybir

ALU = mybir.AluOpType
ACT = mybir.ActivationFunctionType
F32 = mybir.dt.float32
F32R = mybir.dt.float32r
BF16 = mybir.dt.bfloat16
AX = mybir.AxisListType

P = 128
IMAGES = 32
C = 256
J = C // P
H = W = 28
HW = H * W
HALF = HW // 2
EXPERTS = 8
GROUP = C // 32
TAPS = 9
PH, PW = H + 2, W + 2
TOK = 112
M = HW // TOK
ROWS = TOK // W
BAND = (ROWS + 2) * W
WINDOW = 256
BAND_PAD = WINDOW - BAND // 2
UNROLL = 2
STAGES = 7
PARAMS = ["dw_b", "pw_b", "b_ln", "b_v", "bn1_g", "bn1_b", "bn1_m", "bn1_v", "bn2_g", "bn2_b", "bn2_m", "bn2_v"]

GN_EPS = 1e-5
BN_EPS = 1e-5
DW_THRESH = 4.0
PW_THRESH = 0.001
DIV_EPS = 1e-7
NORM_EPS = 1e-12

GN_SQ, GN_VAR, GN_R, GN_DONE = 1, 2, 3, 4


class Image:

    def __init__(self, pair, offset):
        self.pair, self.offset = pair, offset

    def __sub__(self, n):
        return Image(self.pair, self.offset - n)

    def __add__(self, n):
        return Image(self.pair, self.offset + n)

    def times(self, per, more=0):
        if self.pair is None:
            return per * self.offset + more
        return self.pair * (per * UNROLL) + (per * self.offset + more)

    @property
    def odd(self):
        return self.offset % 2

    @property
    def active(self):
        return self.pair is not None or 0 <= self.offset < IMAGES

    @property
    def first(self):
        return self.pair is None and self.offset == 0

    @property
    def started(self):
        return self.pair is not None or self.offset >= 0


class Count:

    def __init__(self, sem, per=1):
        self.sem, self.per = sem, per

    def at(self, image, count=None):
        return image.times(self.per, self.per if count is None else count)


class DmaCount:

    def __init__(self, sems):
        self.sems = sems

    def of(self, image):
        return self.sems[image.odd]

    def at(self, image):
        turn = 16 * (image.offset // 2 + 1)
        return turn if image.pair is None else image.pair * 16 + turn


def build(nc, x, gate_wT, gate_b, expert_wT, dw_w, channel_params, pw_wT, w_qk, b_qk, w_vT, w_ln, group_mean, ident,
          box_band, out):
    with ExitStack() as ctx:
        def sb(name, shape, dt=F32):
            return ctx.enter_context(nc.sbuf_tensor(name, shape, dt))

        def sem(name):
            return ctx.enter_context(nc.semaphore(name))

        def sig(name, per=1):
            return Count(sem(name), per)

        gate_w_sb = sb("gate_w_sb", [P, J, EXPERTS])
        gate_b_sb = sb("gate_b_sb", [P, EXPERTS])
        expert_sb = sb("expert_sb", [P, EXPERTS, J * C])
        dw_sb = sb("dw_sb", [P, J, TAPS])
        params = sb("params", [P, len(PARAMS), J])
        dwb_sb, pwb_sb, bln_sb, bv_col = (params[:, n, :] for n in range(4))
        bn1_sb, bn2_sb = params[:, 4:8, :], params[:, 8:12, :]
        pw_sb = sb("pw_sb", [P, J, C])
        wqk = sb("wqk", [P, 2, J, 2 * C], F32R)
        w_out = sb("w_out", [P, 2, J, C], F32R)
        gmean = sb("gmean", [P, P])
        idn = sb("idn", [P, P])
        band = sb("band", [TOK, BAND + 2 * BAND_PAD], F32R)
        ones = sb("ones", [P, P])
        ones3 = sb("ones3", [3, TOK], BF16)
        bqk3 = sb("bqk3", [3, 2 * C], BF16)
        bn_scale = sb("bn_scale", [P, 2, J])
        bn_shift = sb("bn_shift", [P, 2, J])
        bn_tmp = sb("bn_tmp", [P, 2, J])
        qk_mean = sb("qk_mean", [P, J, 2])
        bqk_mean = sb("bqk_mean", [1, 2])
        b_out = sb("b_out", [P, J])
        bv_ln = sb("bv_ln", [1, C])

        x0 = sb("x0", [P, 2, J, HW])
        xn03 = sb("xn03", [P, J, HW])
        mixed = sb("mixed", [P, J * C])
        mix_tmp = sb("mix_tmp", [P, 2, J * C])
        x1 = sb("x1", [P, 2, J, HW])
        xpad = sb("xpad", [P, J, PH, PW])
        h = sb("h", [P, 2, J, HW])
        pw_masked = sb("pw_masked", [P, J, C])
        x2 = sb("x2", [P, 2, J, HW])
        xn2 = sb("xn2", [P, J, HW])
        xn2_parts = sb("xn2_parts", [P, 2, J, HW], F32R)
        q2 = sb("q2", [TOK, M, C])
        k2 = sb("k2", [TOK, M, C])
        junk = sb("junk", [P, M * C], BF16)
        ksq = sb("ksq", [TOK, 2, C])
        ksum = sb("ksum", [TOK, 2, C])
        xT = sb("xT", [TOK, M, C])
        kx_parts = sb("kx_parts", [P, 2, J, C], F32R)
        attn_parts = sb("attn_parts", [P, 2, J, C], F32R)
        qT_parts = sb("qT_parts", [P, 2, J, HW], F32R)
        x3 = sb("x3", [P, 2, J, HW])
        x3T_parts = sb("x3T_parts", [TOK, 2, M, C], F32R)

        wqk_raw = x3[:, 0].rearrange("p j n -> p (j n)")[:, 0:J * 2 * C].rearrange("p (j n) -> p j n", j=J)
        wv_ln = x3[:, 1].rearrange("p j n -> p (j n)")[:, 0:2 * J * C].rearrange("p (w j n) -> p w j n", w=2, j=J)
        wvT_sb, wln_sb = wv_ln[:, 0], wv_ln[:, 1]
        bias_rows = xn2[0:1].rearrange("p j n -> p (j n)")[:, 0:3 * 2 * C].rearrange("p (k n) -> p k n", k=3)
        bqk_row, bqk_rest = bias_rows[:, 0, :], bias_rows[:, 1:3, :]
        bqk_parts = xT[0:1].rearrange("p m c -> p (m c)")[:, 0:3 * C].bitcast(BF16).rearrange("p (k n) -> p k n", k=3)
        box_raw = q2[:, 0, 0:BAND]

        gn_in = sb("gn_in", [P, 4, 4])
        gn_avg = sb("gn_avg", [P, 4, 4])
        gn_sq = sb("gn_sq", [P, 4, J])
        gn_var = sb("gn_var", [P, 4, J])
        gn_sd = sb("gn_sd", [P, 4, J])
        gn_r = sb("gn_r", [P, 4, J])
        gn_s = sb("gn_s", [P, 4, J])
        pooled = sb("pooled", [P, 2, J])
        gate_in = sb("gate_in", [P, J, EXPERTS])
        z = sb("z", [P, EXPERTS])
        zz = sb("zz", [P, 2, EXPERTS, EXPERTS])
        excess = sb("excess", [P, EXPERTS])
        support = sb("support", [P, 2, EXPERTS])
        tau = sb("tau", [P, 4])
        gate = sb("gate", [P, EXPERTS])
        hmax = sb("hmax", [P, J])
        hmask = sb("hmask", [P, J])
        ymax = sb("ymax", [P, J])
        ymask = sb("ymask", [P, J])
        qk_sum = sb("qk_sum", [TOK, 2, M])
        qk_rec = sb("qk_rec", [TOK, 2, M])
        q_nsq = sb("q_nsq", [TOK, M])
        q_norm = sb("q_norm", [TOK, M])
        q_alpha = sb("q_alpha", [TOK, 3, M])
        k_norm = sb("k_norm", [P, J])
        k_inv = sb("k_inv", [P, 2, J])
        k_row = sb("k_row", [1, C])

        conv_ps = ctx.enter_context(nc.psum_tensor("conv_ps", [P, 4, 512], F32))
        tile_ps = ctx.enter_context(nc.psum_tensor("tile_ps", [P, 3, 512], F32))
        small_ps = ctx.enter_context(nc.psum_tensor("small_ps", [P, 512], F32))

        held = {name: sem(f"held_{name}") for name in ("dve", "pool", "sp")}

        def hold(eng, name):
            eng.sem_inc(held[name], 1)

        gate_loaded = sem("gate_loaded")
        w_loaded = sem("w_loaded")
        experts_loaded = sem("experts_loaded")
        setup_dve = sem("setup_dve")
        setup_act = sem("setup_act")
        setup_pe = sem("setup_pe")
        setup_pool = sem("setup_pool")
        bias_moved = sem("bias_moved")
        x_loaded = DmaCount([sem("x_loaded_even"), sem("x_loaded_odd")])
        stored = DmaCount([sem("stored_even"), sem("stored_odd")])
        gn = sig("gn", GN_DONE)
        gn_sums = [sig(f"gn_sums{n}", 2 * J if n == 0 else J) for n in range(4)]
        gn_mm = sig("gn_mm")
        gn_read = sig("gn_read")
        gn_sqrt = sig("gn_sqrt")
        xn0_ready = sig("xn0_ready", J)
        gate_step = sig("gate_step", 14)
        gate_mm = sig("gate_mm")
        mix_step = sig("mix_step", 2 * EXPERTS - 1)
        conv0_mm = sig("conv0_mm", J)
        x1_ready = sig("x1_ready", J)
        xpad_ready = sig("xpad_ready", J)
        dw_step = sig("dw_step", J * TAPS)
        h_ready = sig("h_ready", J)
        hmask_step = sig("hmask_step", 2)
        pw_masked_ready = sig("pw_masked_ready", J)
        pw_mm = sig("pw_mm", J)
        y_ready = sig("y_ready", J)
        ymask_step = sig("ymask_step", 2)
        x2_ready = sig("x2_ready", J)
        xn2_ready = sig("xn2_ready", J)
        xn2_hi = sig("xn2_hi", J)
        xn2_lo = sig("xn2_lo", J)
        qk_mm = sig("qk_mm", M)
        q2_ready = sig("q2_ready", M)
        k2_ready = sig("k2_ready", M)
        rec_step = sig("rec_step", 2)
        kn_ready = sig("kn_ready", M)
        q4_ready = sig("q4_ready", M)
        q_root = sig("q_root")
        alpha_step = sig("alpha_step", 3)
        qa_ready = sig("qa_ready", M)
        ksum_step = sig("ksum_step", 3 * M - 2)
        xT_mm = sig("xT_mm", 4)
        xT_ready = sig("xT_ready", 4)
        kx_mm = sig("kx_mm")
        kx_hi = sig("kx_hi")
        kx_lo = sig("kx_lo")
        ksum_mm = sig("ksum_mm")
        ksum_read = sig("ksum_read", 2)
        kinv_step = sig("kinv_step", 2)
        attn_w_mm = sig("attn_w_mm")
        attn_hi = sig("attn_hi", J)
        attn_lo = sig("attn_lo", J)
        qT_mm = sig("qT_mm", 4)
        qT_hi = sig("qT_hi", 4)
        qT_lo = sig("qT_lo", 4)
        value_mm = sig("value_mm")
        attn_mm = sig("attn_mm", J)
        x3_ready = sig("x3_ready", J)
        xn3_ready = sig("xn3_ready", J)
        x3T_mm = sig("x3T_mm", 4)
        x3T_hi = sig("x3T_hi", 4)
        x3T_lo = sig("x3T_lo", 4)
        box_mm = sig("box_mm", J)
        x4_ready = sig("x4_ready", J)

        x_dram = x.rearrange("b (j p) h w -> b p j (h w)", p=P)
        out_dram = out.rearrange("b (j p) h w -> b p j (h w)", p=P)

        def half(j):
            return slice(j * P, (j + 1) * P)

        def split(tile):
            return tile.rearrange("p (a n) -> p a n", a=2)

        def conv_banks(j):
            return conv_ps[:, 2 * j:2 * j + 2, 0:HALF]

        def run(eng, step):
            first, last = 8, IMAGES - 2
            for t in range(-1, first):
                step(Image(None, t))
            with eng.Fori(first // UNROLL, last // UNROLL) as pair:
                for u in range(UNROLL):
                    step(Image(pair, u))
            for t in range(last, IMAGES + STAGES - 2):
                step(Image(None, t))

        PAIRS = [[2 * b, 2 * b + 1] if 2 * b + 1 < M else [2 * b] for b in range(4)]
        QUADS = [(j, ms) for j in range(J) for ms in ([0, 1, 2, 3], [4, 5, 6])]
        BOX = []
        for a in range(2):
            parts = []
            for m in range(M):
                lo, hi = max(m * TOK - W, a * HALF), min(m * TOK + TOK + W, (a + 1) * HALF)
                if lo < hi:
                    dst = min(lo - a * HALF, HALF - WINDOW)
                    parts.append((m, dst, a * HALF + dst - (m * TOK - W) + BAND_PAD))
            BOX.append(parts)

        block = ctx.enter_context(nc.Block())

        gate_loads = [
            (gmean[:], group_mean),
            (gate_w_sb[:], gate_wT.rearrange("(j p) k -> p j k", p=P)),
            (gate_b_sb[:], gate_b[None, :].to_broadcast([P, EXPERTS])),
        ]
        loads = [
            (params[:], channel_params),
            (bqk_row, b_qk[None, :]),
            (wqk_raw, w_qk.rearrange("(j p) o -> p j o", p=P)),
            (wvT_sb, w_vT.rearrange("(j p) o -> p j o", p=P)),
            (wln_sb, w_ln.rearrange("(j p) o -> p j o", p=P)),
            (box_raw, box_band),
            (dw_sb[:], dw_w.rearrange("(j p) a b c -> p j (a b c)", p=P)),
            (idn[:], ident),
            (pw_sb[:], pw_wT.rearrange("(j p) o -> p j o", p=P)),
        ]
        GATE_LOADED, LOADED, EXPERTS_LOADED = 16 * len(gate_loads), 16 * len(loads), 16 * EXPERTS

        @block.sync
        def _(sp):
            sp.dma_start(x0[:, 0], x_dram[0]).then_inc(x_loaded.sems[0], 16)
            for dst, src in gate_loads:
                sp.dma_start(dst, src).then_inc(gate_loaded, 16)
            for dst, src in loads:
                sp.dma_start(dst, src).then_inc(w_loaded, 16)
            for k in range(EXPERTS):
                sp.dma_start(expert_sb[:, k, :].rearrange("p (j o) -> p j o", j=J),
                             expert_wT[k].rearrange("(j p) o -> p j o", p=P)).then_inc(experts_loaded, 16)

            def step(t):
                Z, F = t + 1, t - 5
                if Z.active and (Z.pair is not None or Z.offset > 0):
                    if (Z - 2).active:
                        sp.wait_ge(x1_ready.sem, x1_ready.at(Z - 2))
                        hold(sp, "sp")
                    sp.dma_start(x0[:, Z.odd], x_dram[Z.times(1)]).then_inc(x_loaded.of(Z), 16)
                if F.active:
                    sp.wait_ge(x4_ready.sem, x4_ready.at(F))
                    sp.dma_start(out_dram[F.times(1)], x3[:, F.odd]).then_inc(stored.of(F), 16)

            run(sp, step)
            for last in (Image(None, IMAGES - 2), Image(None, IMAGES - 1)):
                sp.wait_ge(stored.of(last), stored.at(last))

        @block.tensor
        def _(pe):
            def setup():
                pe.wait_ge(w_loaded, LOADED)
                for i in range(J):
                    for d in range(J):
                        mm = nc.tensor.matmul(tile_ps[:, 0, i * C:(i + 1) * C], wvT_sb[:, d, half(i)],
                                              wln_sb[:, d, :], start=(d == 0), stop=(d == J - 1))
                mm.then_inc(setup_pe, 1)
                for o in range(J):
                    for d in range(J):
                        mm = nc.tensor.matmul(tile_ps[:, 1, o:o + 1], wln_sb[:, d, half(o)], bv_col[:, d:d + 1],
                                              start=(d == 0), stop=(d == J - 1))
                for d in range(J):
                    mm = nc.tensor.matmul(tile_ps[0:1, 2, 0:C], bv_col[:, d:d + 1], wln_sb[:, d, :],
                                          start=(d == 0), stop=(d == J - 1))
                mm.then_inc(setup_pe, 1)

            def setup_done():
                pe.wait_ge(setup_dve, SETUP_DVE)
                pe.wait_ge(bias_moved, 48)

            pe.wait_ge(gate_loaded, GATE_LOADED)
            pe.wait_ge(setup_pool, SETUP_POOL)

            def wait_free(*readers):
                for img, count, k in readers:
                    if img.active:
                        pe.wait_ge(count.sem, count.at(img, k))
                        return

            def group_means(Z, A, C_, E):
                if A.active:
                    pe.wait_ge(gate_step.sem, gate_step.at(A, 4))
                elif A.started:
                    pe.wait_ge(gn_read.sem, gn_read.at(A))
                if Z.active:
                    pe.wait_ge(gn_sums[0].sem, gn_sums[0].at(Z))
                for img, layer, made in ((A, 1, x1_ready), (C_, 2, x2_ready), (E, 3, x3_ready)):
                    if img.active:
                        pe.wait_ge(made.sem, made.at(img))
                        pe.wait_ge(gn_sums[layer].sem, gn_sums[layer].at(img))
                nc.tensor.matmul(small_ps[:, 0:16], gmean[:], gn_in[:].rearrange("p l n -> p (l n)"), start=True,
                                 stop=True).then_inc(gn_mm.sem, 1)

            def gate_logits(A):
                pe.wait_ge(gn_read.sem, gn_read.at(A))
                pe.wait_ge(gate_step.sem, gate_step.at(A, 3))
                for j in range(J):
                    mm = nc.tensor.matmul(small_ps[:, 0:EXPERTS], ones[:], gate_in[:, j, :], start=(j == 0),
                                          stop=(j == J - 1))
                mm.then_inc(gate_mm.sem, 1)

            def conv_tile(j, parts, first=True, last=True):
                for i, (wt, act) in enumerate(parts):
                    for a in range(2):
                        mm = nc.tensor.matmul(conv_ps[:, 2 * j + a, 0:HALF], wt[:, half(j)],
                                              act[:, a * HALF:(a + 1) * HALF],
                                              start=(first and i == 0), stop=(last and i == len(parts) - 1),
                                              skip_group_check=True)
                return mm

            def by_parts(wt, act):
                return [(wt[:, u, i, :], act[:, v, i, :]) for i in range(J) for u, v in ((0, 0), (0, 1), (1, 0))]

            def q_to_channels(E, banks):
                pe.wait_ge(qa_ready.sem, qa_ready.at(E))
                before = [[], [], [(E, kx_lo, 1)], [(E, qT_lo, 1)]]
                for n in banks:
                    j, ms = QUADS[n]
                    wait_free(*before[n])
                    for s, m in enumerate(ms):
                        mm = nc.tensor.transpose(tile_ps[:, QT_BANK[n], s * TOK:(s + 1) * TOK], q2[:, m, half(j)],
                                                 idn[0:TOK, 0:TOK])
                    mm.then_inc(qT_mm.sem, 1)

            def to_tokens(b, bank, source):
                for s, m in enumerate(PAIRS[b]):
                    for i in range(J):
                        mm = nc.tensor.transpose(tile_ps[0:TOK, bank, s * C + i * P:s * C + (i + 1) * P],
                                                 source[:, i, m * TOK:(m + 1) * TOK], idn[:])
                return mm

            def x3_to_tokens(F, E):
                pe.wait_ge(xn3_ready.sem, xn3_ready.at(F))
                before = [[(E, qT_lo, 3)], [(E, qT_lo, 4)], [(E, ksum_read, 2), (F, ksum_read, 2)], [(F, x3T_lo, 1)]]
                for b in range(4):
                    wait_free(*before[b])
                    to_tokens(b, X3T_BANK[b], xn03).then_inc(x3T_mm.sem, 1)

            def key_sums(E):
                wait_free((E, qT_lo, 2))
                pe.wait_ge(ksum_step.sem, ksum_step.at(E))
                bank = tile_ps[:, KSUM_BANK, :]
                nc.tensor.matmul(bank[0:1, 0:C], ones[0:TOK, 0:1], ksum[:, 0, :], start=True, stop=True)
                for c in range(J):
                    mm = nc.tensor.matmul(bank[:, C + c:C + c + 1], ksum[:, 1, half(c)], ones[0:TOK, 0:1],
                                          start=True, stop=True)
                mm.then_inc(ksum_mm.sem, 1)

            def attention_weights(E, F):
                wait_free((F, x3T_lo, 2), (E, qT_lo, 4))
                pe.wait_ge(kx_lo.sem, kx_lo.at(E))
                pe.wait_ge(ksum_read.sem, ksum_read.at(E))
                for c in range(J):
                    dst = tile_ps[:, ATTN_BANK, c * C:(c + 1) * C]
                    nc.tensor.matmul(dst, k_row[:, half(c)], bv_ln[:], start=True, stop=False)
                    for i in range(J):
                        for u, v in ((0, 0), (0, 1), (1, 0)):
                            mm = nc.tensor.matmul(dst, kx_parts[:, u, i, half(c)], w_out[:, v, i, :], start=False,
                                                  stop=(i == J - 1 and u == 1))
                mm.then_inc(attn_w_mm.sem, 1)

            def value_out(B, D, E, F):
                for j in range(J):
                    wait_free((B, x1_ready, j + 1), (D, y_ready, j + 1), (F - 1, x4_ready, j + 1))
                    mm = conv_tile(j, by_parts(w_out, xn2_parts), last=False)
                mm.then_inc(value_mm.sem, 1)

            def attention_out(E):
                pe.wait_ge(attn_lo.sem, attn_lo.at(E))
                pe.wait_ge(qT_lo.sem, qT_lo.at(E))
                for j in range(J):
                    conv_tile(j, by_parts(attn_parts, qT_parts), first=False).then_inc(attn_mm.sem, 1)

            def pointwise(C_):
                pe.wait_ge(h_ready.sem, h_ready.at(C_))
                pe.wait_ge(pw_masked_ready.sem, pw_masked_ready.at(C_))
                for j in range(J):
                    wait_free((C_ - 3, x4_ready, j + 1), (C_ - 2, x3_ready, j + 1), (C_ + 1, x1_ready, j + 1))
                    conv_tile(j, [(pw_masked[:, i, :], h[:, C_.odd, i, :]) for i in range(J)]).then_inc(pw_mm.sem, 1)

            def box_sums(F):
                pe.wait_ge(x3T_lo.sem, x3T_lo.at(F))
                for j in range(J):
                    wait_free((F + 1, x3_ready, j + 1), (F - 1, x4_ready, j + 1))
                    for a in range(2):
                        for i, (m, dst, src) in enumerate(BOX[a]):
                            for u in range(2):
                                mm = nc.tensor.matmul(conv_ps[:, 2 * j + a, dst:dst + WINDOW],
                                                      x3T_parts[:, u, m, half(j)], band[:, src:src + WINDOW],
                                                      start=(i == 0 and u == 0),
                                                      stop=(i == len(BOX[a]) - 1 and u == 1), skip_group_check=True)
                    mm.then_inc(box_mm.sem, 1)

            def queries_keys(D):
                pe.wait_ge(xn2_lo.sem, xn2_lo.at(D))
                before = [[(D - 1, attn_lo, J)], [(D, xT_ready, 3)], [(D, xT_ready, 4)]
                          ] + [[(D, k2_ready, m - 2)] for m in range(3, M)]
                for m in range(M):
                    wait_free(*before[m])
                    bank = tile_ps[0:TOK, QK_BANK[m], :]
                    nc.tensor.matmul(bank, ones3[:], bqk3[:], start=True, stop=False)
                    for i in range(J):
                        for u, v in ((0, 0), (0, 1), (1, 0)):
                            mm = nc.tensor.matmul(bank, xn2_parts[:, u, i, m * TOK:(m + 1) * TOK], wqk[:, v, i, :],
                                                  start=False, stop=(i == J - 1 and u == 1))
                    mm.then_inc(qk_mm.sem, 1)

            def x2_to_tokens(D, E, F):
                pe.wait_ge(xn2_ready.sem, xn2_ready.at(D))
                before = [[(F, x3T_lo, 3), (E, ksum_read, 2)], [(F, x3T_lo, 4), (E, qT_lo, 3)], [(D, xT_ready, 1)],
                          [(D, xT_ready, 2)]]
                for b in range(4):
                    wait_free(*before[b])
                    to_tokens(b, XT_BANK[b], xn2).then_inc(xT_mm.sem, 1)

            def mixed_conv(A):
                pe.wait_ge(xn0_ready.sem, xn0_ready.at(A))
                pe.wait_ge(mix_step.sem, mix_step.at(A))
                for j in range(J):
                    wait_free((A - 2, y_ready, j + 1), (A - 1, x1_ready, j + 1))
                    conv_tile(j, [(mixed[:, i * C:(i + 1) * C], xn03[:, i, :]) for i in range(J)]
                              ).then_inc(conv0_mm.sem, 1)

            def keys_x(D):
                pe.wait_ge(kn_ready.sem, kn_ready.at(D))
                pe.wait_ge(xT_ready.sem, xT_ready.at(D))
                for i in range(J):
                    for m in range(M):
                        mm = nc.tensor.matmul(tile_ps[:, KX_BANK, i * C:(i + 1) * C], xT[:, m, half(i)], k2[:, m, :],
                                              start=(m == 0), stop=(m == M - 1))
                mm.then_inc(kx_mm.sem, 1)

            def step(t):
                Z, A, B, C_, D, E, F = (t + 1 - n for n in range(STAGES))
                if E.active:
                    value_out(B, D, E, F)
                    q_to_channels(E, range(3))
                if A.active:
                    gate_logits(A)
                if t.first:
                    setup()
                if E.active:
                    q_to_channels(E, range(3, 4))
                    key_sums(E)
                if F.active:
                    x3_to_tokens(F, E)
                if E.active:
                    attention_weights(E, F)
                if D.active:
                    x2_to_tokens(D, E, F)
                if E.active:
                    attention_out(E)
                if D.active:
                    queries_keys(D)
                if F.active:
                    box_sums(F)
                if C_.active:
                    pointwise(C_)
                if A.active:
                    mixed_conv(A)
                if t.first:
                    setup_done()
                if D.active:
                    keys_x(D)
                if t.pair is not None or t.offset < IMAGES + STAGES - 3:
                    group_means(Z, A, C_, E)

            run(pe, step)

        @block.vector
        def _(dve):
            setup = [0]

            def did(ins):
                ins.then_inc(setup_dve, 1)
                setup[0] += 1
                dve.wait_ge(setup_dve, setup[0])

            def parts_of(dst, source):
                did(nc.vector.tensor_copy(dst[:, 0], source))
                did(nc.vector.tensor_tensor(dst[:, 1], source, dst[:, 0].bitcast(F32), ALU.subtract))

            dve.wait_ge(gate_loaded, GATE_LOADED)

            def setup_weights():
                dve.wait_ge(w_loaded, LOADED)
                for j in range(J):
                    for s in range(2):
                        cols = slice(s * C, (s + 1) * C)
                        did(nc.vector.tensor_reduce(qk_mean[:, j, s:s + 1], wqk_raw[:, j, cols], AX.X, ALU.add))
                        did(nc.vector.tensor_scalar(qk_mean[:, j, s:s + 1], qk_mean[:, j, s:s + 1], 1.0 / C, None, ALU.mult))
                        did(nc.vector.tensor_scalar(wqk_raw[:, j, cols], wqk_raw[:, j, cols], qk_mean[:, j, s:s + 1], None,
                                                    ALU.subtract))
                for s in range(2):
                    cols = slice(s * C, (s + 1) * C)
                    did(nc.vector.tensor_reduce(bqk_mean[:, s:s + 1], bqk_row[:, cols], AX.X, ALU.add))
                    did(nc.vector.tensor_scalar(bqk_mean[:, s:s + 1], bqk_mean[:, s:s + 1], 1.0 / C, None, ALU.mult))
                    did(nc.vector.tensor_scalar(bqk_row[:, cols], bqk_row[:, cols], bqk_mean[:, s:s + 1], None,
                                                ALU.subtract))
                did(nc.vector.tensor_copy(bqk_parts[:, 0, :], bqk_row))
                did(nc.vector.tensor_tensor(bqk_rest[:, 0, :], bqk_row, bqk_parts[:, 0, :], ALU.subtract))
                did(nc.vector.tensor_copy(bqk_parts[:, 1, :], bqk_rest[:, 0, :]))
                did(nc.vector.tensor_tensor(bqk_rest[:, 1, :], bqk_rest[:, 0, :], bqk_parts[:, 1, :], ALU.subtract))
                did(nc.vector.tensor_copy(bqk_parts[:, 2, :], bqk_rest[:, 1, :]))
                for n, (bn, bias) in enumerate(((bn1_sb, dwb_sb), (bn2_sb, pwb_sb))):
                    did(nc.vector.tensor_scalar(bn_tmp[:, n, :], bn[:, 3, :], BN_EPS, None, ALU.add))
                dve.wait_ge(setup_act, 1)
                for n, (bn, bias) in enumerate(((bn1_sb, dwb_sb), (bn2_sb, pwb_sb))):
                    did(nc.vector.reciprocal(bn_scale[:, n, :], bn_shift[:, n, :]))
                    did(nc.vector.tensor_tensor(bn_scale[:, n, :], bn_scale[:, n, :], bn[:, 0, :], ALU.mult))
                    did(nc.vector.tensor_tensor(bn_tmp[:, n, :], bias, bn[:, 2, :], ALU.subtract))
                    did(nc.vector.tensor_tensor(bn_tmp[:, n, :], bn_tmp[:, n, :], bn_scale[:, n, :], ALU.mult))
                    did(nc.vector.tensor_tensor(bn_shift[:, n, :], bn_tmp[:, n, :], bn[:, 1, :], ALU.add))
                parts_of(wqk, wqk_raw)
                dve.wait_ge(setup_pool, SETUP_POOL)
                did(nc.vector.tensor_copy(band[:, BAND_PAD:BAND_PAD + BAND], box_raw))
                dve.wait_ge(setup_pe, 2)
                parts_of(w_out, tile_ps[:, 0, :].rearrange("p (i c) -> p i c", i=J))
                did(nc.vector.tensor_tensor(b_out[:], tile_ps[:, 1, 0:J], bln_sb, ALU.add))
                did(nc.vector.tensor_copy(bv_ln[:], tile_ps[0:1, 2, 0:C]))
                assert setup[0] == SETUP_DVE

            def variances(A):
                dve.wait_ge(gn_mm.sem, gn_mm.at(A))
                nc.vector.tensor_copy(gn_avg[:].rearrange("p l n -> p (l n)"), small_ps[:, 0:16]
                                      ).then_inc(gn_read.sem, 1)
                dve.wait_ge(gn_read.sem, gn_read.at(A))
                mean, mean_sq = gn_avg[:, :, 0:2], gn_avg[:, :, 2:4]
                nc.vector.tensor_tensor(gn_sq[:], mean, mean, ALU.mult).then_inc(gn.sem, 1)
                dve.wait_ge(gn.sem, gn.at(A, GN_SQ))
                nc.vector.scalar_tensor_tensor(gn_var[:], mean_sq, GN_EPS, gn_sq[:], ALU.add,
                                               ALU.subtract).then_inc(gn.sem, 1)

            def scales_shifts(A):
                dve.wait_ge(gn_sqrt.sem, gn_sqrt.at(A))
                nc.vector.reciprocal(gn_r[:], gn_sd[:]).then_inc(gn.sem, 1)
                dve.wait_ge(gn.sem, gn.at(A, GN_R))
                nc.vector.scalar_tensor_tensor(gn_s[:], gn_avg[:, :, 0:2], -1.0, gn_r[:], ALU.mult,
                                               ALU.mult).then_inc(gn.sem, 1)

            def gate_logits(A):
                s = gate_step
                dve.wait_ge(gn.sem, gn.at(A))
                nc.vector.scalar_tensor_tensor(pooled[:, 0, :], gn_in[:, 0, 0:2], 1.0 / HW, gn_r[:, 0, :], ALU.mult,
                                               ALU.mult).then_inc(s.sem, 1)
                dve.wait_ge(s.sem, s.at(A, 1))
                nc.vector.tensor_tensor(pooled[:, 1, :], pooled[:, 0, :], gn_s[:, 0, :], ALU.add).then_inc(s.sem, 1)
                dve.wait_ge(s.sem, s.at(A, 2))
                nc.vector.tensor_tensor(gate_in[:], gate_w_sb[:],
                                        pooled[:, 1, :].unsqueeze(2).to_broadcast([P, J, EXPERTS]),
                                        ALU.mult).then_inc(s.sem, 1)

            def sparsemax(A):
                s = gate_step
                dve.wait_ge(gate_mm.sem, gate_mm.at(A))
                nc.vector.tensor_tensor(z[:], small_ps[:, 0:EXPERTS], gate_b_sb[:], ALU.add).then_inc(s.sem, 1)
                dve.wait_ge(s.sem, s.at(A, 4))
                nc.vector.tensor_tensor(zz[:, 0], z[:].unsqueeze(1).to_broadcast([P, EXPERTS, EXPERTS]),
                                        z[:].unsqueeze(2).to_broadcast([P, EXPERTS, EXPERTS]),
                                        ALU.subtract).then_inc(s.sem, 1)
                dve.wait_ge(s.sem, s.at(A, 5))
                nc.vector.tensor_scalar(zz[:, 1], zz[:, 0], 0.0, None, ALU.max).then_inc(s.sem, 1)
                dve.wait_ge(s.sem, s.at(A, 6))
                nc.vector.tensor_reduce(excess[:], zz[:, 1], AX.X, ALU.add).then_inc(s.sem, 1)
                dve.wait_ge(s.sem, s.at(A, 7))
                nc.vector.tensor_scalar(support[:, 0, :], excess[:], 1.0, None, ALU.is_lt).then_inc(s.sem, 1)
                dve.wait_ge(s.sem, s.at(A, 8))
                nc.vector.tensor_tensor(support[:, 1, :], support[:, 0, :], z[:], ALU.mult).then_inc(s.sem, 1)
                dve.wait_ge(s.sem, s.at(A, 9))
                nc.vector.tensor_reduce(tau[:, 0:2], support[:], AX.X, ALU.add).then_inc(s.sem, 1)
                dve.wait_ge(s.sem, s.at(A, 10))
                nc.vector.reciprocal(tau[:, 2:3], tau[:, 0:1]).then_inc(s.sem, 1)
                nc.vector.tensor_scalar(tau[:, 1:2], tau[:, 1:2], -1.0, None, ALU.add).then_inc(s.sem, 1)
                dve.wait_ge(s.sem, s.at(A, 12))
                nc.vector.tensor_tensor(tau[:, 3:4], tau[:, 1:2], tau[:, 2:3], ALU.mult).then_inc(s.sem, 1)
                dve.wait_ge(s.sem, s.at(A, 13))
                if (A - 1).active:
                    dve.wait_ge(mix_step.sem, mix_step.at(A - 1))
                nc.vector.tensor_scalar(gate[:], z[:], tau[:, 3:4], 0.0, ALU.subtract, ALU.max).then_inc(s.sem, 1)

            def depthwise(B, j, taps):
                dve.wait_ge(xpad_ready.sem, xpad_ready.at(B, j + 1))
                if (B - 2).active:
                    dve.wait_ge(pw_mm.sem, pw_mm.at(B - 2))
                acc = h[:, B.odd, j, :].rearrange("p (h w) -> p h w", w=W)
                for tap in taps:
                    view = xpad[:, j, tap // 3:tap // 3 + H, tap % 3:tap % 3 + W]
                    scalar = dw_sb[:, j, tap:tap + 1]
                    if tap == 0:
                        ins = nc.vector.tensor_scalar(acc, view, scalar, None, ALU.mult)
                    else:
                        dve.wait_ge(dw_step.sem, dw_step.at(B, j * TAPS + tap))
                        ins = nc.vector.scalar_tensor_tensor(acc, view, scalar, acc, ALU.mult, ALU.add)
                    ins.then_inc(dw_step.sem, 1)

            def h_mask(B):
                dve.wait_ge(h_ready.sem, h_ready.at(B))
                nc.vector.tensor_reduce(hmax[:], h[:, B.odd], AX.X, ALU.max).then_inc(hmask_step.sem, 1)
                dve.wait_ge(hmask_step.sem, hmask_step.at(B, 1))
                if (B - 1).active:
                    dve.wait_ge(pw_masked_ready.sem, pw_masked_ready.at(B - 1))
                nc.vector.tensor_scalar(hmask[:], hmax[:], DW_THRESH, None, ALU.is_ge).then_inc(hmask_step.sem, 1)

            def make_x2(C_):
                dve.wait_ge(y_ready.sem, y_ready.at(C_))
                nc.vector.tensor_reduce(ymax[:], x2[:, C_.odd], AX.X, ALU.max).then_inc(ymask_step.sem, 1)
                dve.wait_ge(ymask_step.sem, ymask_step.at(C_, 1))
                nc.vector.tensor_scalar(ymask[:], ymax[:], PW_THRESH, None, ALU.is_ge).then_inc(ymask_step.sem, 1)
                dve.wait_ge(ymask_step.sem, ymask_step.at(C_, 2))
                for j in range(J):
                    y = x2[:, C_.odd, j, :]
                    nc.vector.scalar_tensor_tensor(y, y, ymask[:, j:j + 1], x1[:, C_.odd, j, :], ALU.mult, ALU.add,
                                                   accum_out=gn_in[:, 2, j:j + 1]).then_inc(x2_ready.sem, 1)

            def make_x1(A):
                if (A - 2).active:
                    dve.wait_ge(x2_ready.sem, x2_ready.at(A - 2))
                for j in range(J):
                    dve.wait_ge(conv0_mm.sem, conv0_mm.at(A, j + 1))
                    nc.vector.scalar_tensor_tensor(split(x1[:, A.odd, j, :]), conv_banks(j), 1.0,
                                                   split(x0[:, A.odd, j, :]), ALU.mult, ALU.add,
                                                   accum_out=gn_in[:, 1, j:j + 1]).then_inc(x1_ready.sem, 1)

            def make_x3(E):
                if (E - 2).active:
                    dve.wait_ge(stored.of(E - 2), stored.at(E - 2))
                for j in range(J):
                    dve.wait_ge(attn_mm.sem, attn_mm.at(E, j + 1))
                    nc.vector.scalar_tensor_tensor(split(x3[:, E.odd, j, :]), conv_banks(j), b_out[:, j:j + 1],
                                                   split(x2[:, E.odd, j, :]), ALU.add, ALU.add,
                                                   accum_out=gn_in[:, 3, j:j + 1]).then_inc(x3_ready.sem, 1)

            def make_x4(F):
                for j in range(J):
                    dve.wait_ge(box_mm.sem, box_mm.at(F, j + 1))
                    nc.vector.scalar_tensor_tensor(split(x3[:, F.odd, j, :]), conv_banks(j), 1.0 / TAPS,
                                                   split(x3[:, F.odd, j, :]), ALU.mult,
                                                   ALU.add).then_inc(x4_ready.sem, 1)

            def q_low(E):
                for n, (j, ms) in enumerate(QUADS):
                    cols = slice(ms[0] * TOK, (ms[-1] + 1) * TOK)
                    dve.wait_ge(qT_hi.sem, qT_hi.at(E, n + 1))
                    nc.vector.tensor_tensor(qT_parts[:, 1, j, cols], tile_ps[:, QT_BANK[n], 0:len(ms) * TOK],
                                            qT_parts[:, 0, j, cols].bitcast(F32), ALU.subtract).then_inc(qT_lo.sem, 1)

            def x3T_low(F):
                for b, ms in enumerate(PAIRS):
                    tiles = slice(ms[0], ms[-1] + 1)
                    dve.wait_ge(x3T_hi.sem, x3T_hi.at(F, b + 1))
                    nc.vector.tensor_tensor(x3T_parts[:, 1, tiles, :],
                                            tile_ps[0:TOK, X3T_BANK[b], 0:len(ms) * C].rearrange(
                                                "p (m c) -> p m c", c=C),
                                            x3T_parts[:, 0, tiles, :].bitcast(F32),
                                            ALU.subtract).then_inc(x3T_lo.sem, 1)

            def key_norms(E):
                dve.wait_ge(ksum_read.sem, ksum_read.at(E))
                nc.vector.tensor_scalar(k_inv[:, 0, :], k_norm[:], NORM_EPS, None, ALU.max).then_inc(kinv_step.sem, 1)
                dve.wait_ge(kinv_step.sem, kinv_step.at(E, 1))
                nc.vector.reciprocal(k_inv[:, 1, :], k_inv[:, 0, :]).then_inc(kinv_step.sem, 1)

            def attention_weights_low(E):
                dve.wait_ge(attn_hi.sem, attn_hi.at(E))
                for c in range(J):
                    nc.vector.scalar_tensor_tensor(attn_parts[:, 1, c, :], tile_ps[:, ATTN_BANK, c * C:(c + 1) * C],
                                                   k_inv[:, 1, c:c + 1], attn_parts[:, 0, c, :].bitcast(F32),
                                                   ALU.mult, ALU.subtract).then_inc(attn_lo.sem, 1)

            def normalise_x2(A, D):
                dve.wait_ge(gn.sem, gn.at(A))
                if (D - 1).active:
                    dve.wait_ge(xT_mm.sem, xT_mm.at(D - 1))
                for j in range(J):
                    nc.vector.tensor_scalar(xn2[:, j, :], x2[:, D.odd, j, :], gn_r[:, 2, j:j + 1],
                                            gn_s[:, 2, j:j + 1], ALU.mult, ALU.add).then_inc(xn2_ready.sem, 1)

            def x2_low(D):
                for j in range(J):
                    dve.wait_ge(xn2_hi.sem, xn2_hi.at(D, j + 1))
                    nc.vector.tensor_tensor(xn2_parts[:, 1, j, :], xn2[:, j, :], xn2_parts[:, 0, j, :].bitcast(F32),
                                            ALU.subtract).then_inc(xn2_lo.sem, 1)

            def reciprocal_sums(D):
                dve.wait_ge(k2_ready.sem, k2_ready.at(D))
                nc.vector.tensor_scalar(qk_rec[:], qk_sum[:], DIV_EPS, None, ALU.add).then_inc(rec_step.sem, 1)
                dve.wait_ge(rec_step.sem, rec_step.at(D, 1))
                nc.vector.reciprocal(qk_rec[:], qk_rec[:]).then_inc(rec_step.sem, 1)

            def scale_q(D):
                dve.wait_ge(q_root.sem, q_root.at(D))
                nc.vector.tensor_scalar(q_alpha[:, 0, :], q_norm[:], NORM_EPS, None, ALU.max).then_inc(alpha_step.sem, 1)
                dve.wait_ge(alpha_step.sem, alpha_step.at(D, 1))
                nc.vector.reciprocal(q_alpha[:, 1, :], q_alpha[:, 0, :]).then_inc(alpha_step.sem, 1)
                dve.wait_ge(alpha_step.sem, alpha_step.at(D, 2))
                nc.vector.scalar_tensor_tensor(q_alpha[:, 2, :], q_alpha[:, 1, :], float(HW) ** -0.5, qk_rec[:, 0, :],
                                               ALU.mult, ALU.mult).then_inc(alpha_step.sem, 1)
                dve.wait_ge(alpha_step.sem, alpha_step.at(D, 3))
                for m in range(M):
                    nc.vector.tensor_scalar(q2[:, m, :], q2[:, m, :], q_alpha[:, 2, m:m + 1], None,
                                            ALU.mult).then_inc(qa_ready.sem, 1)

            def kx_low(E):
                dve.wait_ge(kx_hi.sem, kx_hi.at(E))
                nc.vector.tensor_tensor(kx_parts[:, 1], tile_ps[:, KX_BANK, :].rearrange("p (i c) -> p i c", i=J),
                                        kx_parts[:, 0].bitcast(F32), ALU.subtract).then_inc(kx_lo.sem, 1)

            def step(t):
                Z, A, B, C_, D, E, F = (t + 1 - n for n in range(STAGES))
                if E.active:
                    kx_low(E)
                if A.started:
                    variances(A)
                    scales_shifts(A)
                if A.active:
                    gate_logits(A)
                if D.active:
                    normalise_x2(A, D)
                if B.active:
                    depthwise(B, 0, range(2))
                if E.active:
                    q_low(E)
                    key_norms(E)
                if F.active:
                    x3T_low(F)
                if B.active:
                    depthwise(B, 0, range(2, 4))
                if E.active:
                    attention_weights_low(E)
                if A.active:
                    sparsemax(A)
                if t.first:
                    setup_weights()
                if D.active:
                    x2_low(D)
                if B.active:
                    depthwise(B, 0, range(4, TAPS))
                if E.active:
                    make_x3(E)
                if B.active:
                    depthwise(B, 1, range(5))
                if D.active:
                    reciprocal_sums(D)
                if B.active:
                    depthwise(B, 1, range(5, 6))
                if F.active:
                    make_x4(F)
                if B.active:
                    depthwise(B, 1, range(6, TAPS))
                if B.active:
                    h_mask(B)
                if D.active:
                    scale_q(D)
                if C_.active:
                    make_x2(C_)
                if A.active:
                    make_x1(A)

            run(dve, step)

        @block.scalar
        def _(act):
            def setup():
                act.wait_ge(setup_dve, SETUP_BN)
                nc.scalar.activation(bn_shift[:], bn_tmp[:], ACT.Sqrt).then_inc(setup_act, 1)
                for k in range(3):
                    act.dma_start(bqk3[k:k + 1, :], bqk_parts[:, k, :]).then_inc(bias_moved, 16)

            act.wait_ge(setup_pool, SETUP_POOL)

            def junk_free(*writers):
                for img, count in writers:
                    if img.active:
                        act.wait_ge(count.sem, count.at(img))
                        return

            def deviations(A):
                act.wait_ge(gn.sem, gn.at(A, GN_VAR))
                nc.scalar.activation(gn_sd[:], gn_var[:], ACT.Sqrt).then_inc(gn_sqrt.sem, 1)

            def sum_squares(layer, img, source, ready):
                for j in range(J):
                    act.wait_ge(ready.sem, ready.at(img, j + 1))
                    nc.scalar.activation(junk[:, j * HW:(j + 1) * HW], source[:, j, :], ACT.Square,
                                         accum_out=gn_in[:, layer, 2 + j:3 + j]).then_inc(gn_sums[layer].sem, 1)

            def normalise(A, layer, outs, source, signal):
                act.wait_ge(gn.sem, gn.at(A))
                for j in range(J):
                    nc.scalar.activation(outs[j], source[j], ACT.Identity, bias=gn_s[:, layer, j:j + 1],
                                         scale=gn_r[:, layer, j:j + 1]).then_inc(signal.sem, 1)

            def normalise_x3(A, B, F):
                if B.active:
                    act.wait_ge(conv0_mm.sem, conv0_mm.at(B))
                elif (F - 1).active:
                    act.wait_ge(x3T_mm.sem, x3T_mm.at(F - 1))
                normalise(A, 3, [xn03[:, j, :] for j in range(J)], [x3[:, F.odd, j, :] for j in range(J)], xn3_ready)

            def normalise_x0(A, B, F):
                if F.active:
                    act.wait_ge(x3T_mm.sem, x3T_mm.at(F))
                elif B.active:
                    act.wait_ge(conv0_mm.sem, conv0_mm.at(B))
                normalise(A, 0, [xn03[:, j, :] for j in range(J)], [x0[:, A.odd, j, :] for j in range(J)], xn0_ready)

            def x0_sums(Z):
                act.wait_ge(x_loaded.of(Z), x_loaded.at(Z))
                if (Z - 1).active:
                    act.wait_ge(gate_step.sem, gate_step.at(Z - 1, 1))
                for n, (j, func) in enumerate([(j, func) for func in (ACT.Square, ACT.Identity) for j in range(J)]):
                    if n >= J:
                        act.wait_ge(gn_sums[0].sem, gn_sums[0].at(Z, n - J + 1))
                    first = 2 if func == ACT.Square else 0
                    nc.scalar.activation(junk[:, j * HW:(j + 1) * HW], x0[:, Z.odd, j, :], func,
                                         accum_out=gn_in[:, 0, first + j:first + j + 1]).then_inc(gn_sums[0].sem, 1)

            def q_high(E):
                if (E - 1).active:
                    act.wait_ge(attn_mm.sem, attn_mm.at(E - 1))
                for n, (j, ms) in enumerate(QUADS):
                    act.wait_ge(qT_mm.sem, qT_mm.at(E, n + 1))
                    nc.scalar.copy(qT_parts[:, 0, j, ms[0] * TOK:(ms[-1] + 1) * TOK],
                                   tile_ps[:, QT_BANK[n], 0:len(ms) * TOK]).then_inc(qT_hi.sem, 1)

            def copy_tokens(img, banks, mm, ready, dst):
                for b, ms in enumerate(PAIRS):
                    act.wait_ge(mm.sem, mm.at(img, b + 1))
                    nc.scalar.copy(dst[:, ms[0]:ms[-1] + 1, :],
                                   tile_ps[0:TOK, banks[b], 0:len(ms) * C].rearrange("p (m c) -> p m c", c=C)
                                   ).then_inc(ready.sem, 1)

            def key_sums(E):
                act.wait_ge(ksum_mm.sem, ksum_mm.at(E))
                nc.scalar.copy(k_row[:], tile_ps[0:1, KSUM_BANK, 0:C]).then_inc(ksum_read.sem, 1)
                nc.scalar.activation(k_norm[:], tile_ps[:, KSUM_BANK, C:C + J], ACT.Sqrt).then_inc(ksum_read.sem, 1)

            def attention_weights_high(E):
                act.wait_ge(attn_w_mm.sem, attn_w_mm.at(E))
                act.wait_ge(kinv_step.sem, kinv_step.at(E))
                for c in range(J):
                    nc.scalar.activation(attn_parts[:, 0, c, :], tile_ps[:, ATTN_BANK, c * C:(c + 1) * C],
                                         ACT.Identity, scale=k_inv[:, 1, c:c + 1]).then_inc(attn_hi.sem, 1)

            def x2_high(D):
                act.wait_ge(xn2_ready.sem, xn2_ready.at(D))
                if (D - 1).active:
                    act.wait_ge(value_mm.sem, value_mm.at(D - 1))
                for j in range(J):
                    nc.scalar.copy(xn2_parts[:, 0, j, :], xn2[:, j, :]).then_inc(xn2_hi.sem, 1)

            def relu_h(B, j):
                act.wait_ge(dw_step.sem, dw_step.at(B, (j + 1) * TAPS))
                nc.scalar.activation(h[:, B.odd, j, :], h[:, B.odd, j, :], ACT.Relu, bias=bn_shift[:, 0, j:j + 1],
                                     scale=bn_scale[:, 0, j:j + 1]).then_inc(h_ready.sem, 1)

            def relu_y(C_, j):
                if (C_ - 2).active:
                    act.wait_ge(x3_ready.sem, x3_ready.at(C_ - 2))
                act.wait_ge(pw_mm.sem, pw_mm.at(C_, j + 1))
                nc.scalar.activation(split(x2[:, C_.odd, j, :]), conv_banks(j), ACT.Relu,
                                     bias=bn_shift[:, 1, j:j + 1],
                                     scale=bn_scale[:, 1, j:j + 1]).then_inc(y_ready.sem, 1)

            def square_qk(D):
                if (D - 1).active:
                    act.wait_ge(qT_mm.sem, qT_mm.at(D - 1))
                    act.wait_ge(kx_mm.sem, kx_mm.at(D - 1))
                    act.wait_ge(ksum_step.sem, ksum_step.at(D - 1))
                for m in range(M):
                    act.wait_ge(qk_mm.sem, qk_mm.at(D, m + 1))
                    bank = tile_ps[0:TOK, QK_BANK[m], :]
                    nc.scalar.activation(q2[:, m, :], bank[:, 0:C], ACT.Square,
                                         accum_out=qk_sum[:, 0, m:m + 1]).then_inc(q2_ready.sem, 1)
                    nc.scalar.activation(k2[:, m, :], bank[:, C:2 * C], ACT.Square,
                                         accum_out=qk_sum[:, 1, m:m + 1]).then_inc(k2_ready.sem, 1)

            def q_norms(D):
                act.wait_ge(rec_step.sem, rec_step.at(D))
                for m in range(M):
                    nc.scalar.activation(junk[0:TOK, m * C:(m + 1) * C], q2[:, m, :], ACT.Square,
                                         scale=qk_rec[:, 0, m:m + 1],
                                         accum_out=q_nsq[:, m:m + 1]).then_inc(q4_ready.sem, 1)
                act.wait_ge(q4_ready.sem, q4_ready.at(D))
                nc.scalar.activation(q_norm[:], q_nsq[:], ACT.Sqrt).then_inc(q_root.sem, 1)

            def kx_high(E):
                act.wait_ge(kx_mm.sem, kx_mm.at(E))
                if (E - 1).active:
                    act.wait_ge(attn_w_mm.sem, attn_w_mm.at(E - 1))
                nc.scalar.copy(kx_parts[:, 0], tile_ps[:, KX_BANK, :].rearrange("p (i c) -> p i c", i=J)
                               ).then_inc(kx_hi.sem, 1)

            def step(t):
                Z, A, B, C_, D, E, F = (t + 1 - n for n in range(STAGES))
                if E.active:
                    kx_high(E)
                if A.started:
                    deviations(A)
                if F.active:
                    normalise_x3(A, B, F)
                if E.active:
                    q_high(E)
                    key_sums(E)
                if F.active:
                    if (F - 1).active:
                        act.wait_ge(box_mm.sem, box_mm.at(F - 1))
                    copy_tokens(F, X3T_BANK, x3T_mm, x3T_hi, x3T_parts[:, 0])
                if D.active:
                    x2_high(D)
                if E.active:
                    attention_weights_high(E)
                if D.active:
                    if (D - 1).active:
                        act.wait_ge(kx_mm.sem, kx_mm.at(D - 1))
                    copy_tokens(D, XT_BANK, xT_mm, xT_ready, xT)
                if A.active:
                    normalise_x0(A, B, F)
                if t.first:
                    setup()
                if Z.active:
                    x0_sums(Z)
                if D.active:
                    square_qk(D)
                if E.active:
                    junk_free((Z, gn_sums[0]))
                    sum_squares(3, E, x3[:, E.odd], x3_ready)
                if B.active:
                    relu_h(B, 0)
                if D.active:
                    junk_free((E, gn_sums[3]), (Z, gn_sums[0]))
                    q_norms(D)
                if C_.active:
                    relu_y(C_, 0)
                if B.active:
                    relu_h(B, 1)
                if C_.active:
                    relu_y(C_, 1)
                if C_.active:
                    junk_free((D, q4_ready), (E, gn_sums[3]), (Z, gn_sums[0]))
                    sum_squares(2, C_, x2[:, C_.odd], x2_ready)
                if t.first:
                    act.wait_ge(setup_dve, SETUP_DVE)
                if A.active:
                    junk_free((C_, gn_sums[2]), (Z, gn_sums[0]))
                    sum_squares(1, A, x1[:, A.odd], x1_ready)

            run(act, step)

        @block.gpsimd
        def _(pool):
            nc.gpsimd.memset(ones[:], 1.0).then_inc(setup_pool, 1)
            nc.gpsimd.memset(ones3[:], 1.0).then_inc(setup_pool, 1)
            nc.gpsimd.memset(xpad[:], 0.0).then_inc(setup_pool, 1)
            nc.gpsimd.memset(band[:].bitcast(F32), 0.0).then_inc(setup_pool, 1)
            nc.gpsimd.memset(gn_in[:], 0.0).then_inc(setup_pool, 1)

            def normalise_x1(A, B, C_):
                pool.wait_ge(setup_pool, SETUP_POOL)
                pool.wait_ge(gn.sem, gn.at(A))
                if C_.active:
                    pool.wait_ge(dw_step.sem, dw_step.at(C_))
                hold(pool, "pool")
                for j in range(J):
                    nc.gpsimd.tensor_scalar(xpad[:, j, 1:1 + H, 1:1 + W],
                                            x1[:, B.odd, j, :].rearrange("p (h w) -> p h w", w=W),
                                            gn_r[:, 1, j:j + 1], gn_s[:, 1, j:j + 1], ALU.mult,
                                            ALU.add).then_inc(xpad_ready.sem, 1)

            def mask_weights(B):
                if (B - 1).active:
                    pool.wait_ge(pw_mm.sem, pw_mm.at(B - 1))
                pool.wait_ge(w_loaded, LOADED)
                pool.wait_ge(hmask_step.sem, hmask_step.at(B))
                hold(pool, "pool")
                for j in range(J):
                    nc.gpsimd.tensor_scalar(pw_masked[:, j, :], pw_sb[:, j, :], hmask[:, j:j + 1], 0.0, ALU.mult,
                                            ALU.add).then_inc(pw_masked_ready.sem, 1)

            def mix(A):
                pool.wait_ge(experts_loaded, EXPERTS_LOADED)
                if (A - 1).active:
                    pool.wait_ge(conv0_mm.sem, conv0_mm.at(A - 1))
                pool.wait_ge(gate_step.sem, gate_step.at(A))
                hold(pool, "pool")
                done = 0
                for k in range(EXPERTS):
                    dst = mixed[:] if k == 0 else mix_tmp[:, k % 2, :]
                    if k >= 3:
                        pool.wait_ge(mix_step.sem, mix_step.at(A, 2 * (k - 2) + 1))
                        hold(pool, "pool")
                    nc.gpsimd.tensor_scalar(dst, expert_sb[:, k, :], gate[:, k:k + 1], 0.0, ALU.mult,
                                            ALU.add).then_inc(mix_step.sem, 1)
                    done += 1
                    if k:
                        pool.wait_ge(mix_step.sem, mix_step.at(A, done))
                        nc.gpsimd.tensor_tensor(mixed[:], mixed[:], mix_tmp[:, k % 2, :],
                                                ALU.add).then_inc(mix_step.sem, 1)
                        done += 1

            def scale_k(D):
                pool.wait_ge(rec_step.sem, rec_step.at(D))
                hold(pool, "pool")
                for m in range(M):
                    nc.gpsimd.tensor_scalar(k2[:, m, :], k2[:, m, :], qk_rec[:, 1, m:m + 1], 0.0, ALU.mult,
                                            ALU.add).then_inc(kn_ready.sem, 1)

            def sum_k(D):
                if (D - 1).active:
                    pool.wait_ge(ksum_mm.sem, ksum_mm.at(D - 1))
                done = 0
                for m in range(M):
                    pool.wait_ge(kn_ready.sem, kn_ready.at(D, m + 1))
                    if m == 0:
                        nc.gpsimd.tensor_tensor(ksum[:, 1, :], k2[:, 0, :], k2[:, 0, :], ALU.mult).then_inc(
                            ksum_step.sem, 1)
                        done += 1
                        continue
                    if m >= 3:
                        pool.wait_ge(ksum_step.sem, ksum_step.at(D, 3 * (m - 2) + 1))
                    nc.gpsimd.tensor_tensor(ksq[:, m % 2, :], k2[:, m, :], k2[:, m, :], ALU.mult).then_inc(
                        ksum_step.sem, 1)
                    a = k2[:, 0, :] if m == 1 else ksum[:, 0, :]
                    nc.gpsimd.tensor_tensor(ksum[:, 0, :], a, k2[:, m, :], ALU.add).then_inc(ksum_step.sem, 1)
                    done += 2
                    pool.wait_ge(ksum_step.sem, ksum_step.at(D, done))
                    nc.gpsimd.tensor_tensor(ksum[:, 1, :], ksum[:, 1, :], ksq[:, m % 2, :], ALU.add).then_inc(
                        ksum_step.sem, 1)
                    done += 1

            def step(t):
                Z, A, B, C_, D, E, F = (t + 1 - n for n in range(STAGES))
                if B.active:
                    normalise_x1(A, B, C_)
                if A.active:
                    mix(A)
                if D.active:
                    scale_k(D)
                    sum_k(D)
                if B.active:
                    mask_weights(B)

            run(pool, step)


SETUP_PARTS = 12 + 6 + 5
SETUP_BN = SETUP_PARTS + 2
SETUP_DVE = SETUP_BN + 10 + 2 + 1 + 2 + 2
SETUP_POOL = 5
BANKS = [n % 3 for n in range(4 + 1 + 4 + 1)]
QT_BANK, KSUM_BANK, X3T_BANK, ATTN_BANK = BANKS[0:4], BANKS[4], BANKS[5:9], BANKS[9]
XT_BANK, QK_BANK, KX_BANK = [1, 2, 1, 2], [m % 3 for m in range(M)], 2


def kernel(x, L0_conv_gate_w, L0_conv_gate_b, L0_conv_expert_w, L1_conv_dw_w, L1_conv_dw_b, L1_conv_bn1_g,
           L1_conv_bn1_b, L1_conv_bn1_m, L1_conv_bn1_v, L1_conv_pw_w, L1_conv_pw_b, L1_conv_bn2_g, L1_conv_bn2_b,
           L1_conv_bn2_m, L1_conv_bn2_v, L2_conv_Wqkv, L2_conv_bqkv, L2_conv_Wln, L2_conv_bln):
    import numpy as np
    import concourse.bacc as bacc
    from concourse.bass_utils import run_bass_kernel_spmd

    c = np.arange(P)
    group_mean = ((c[:, None] // GROUP) == (c[None, :] // GROUP)).astype(np.float32) / (GROUP * HW)
    tok, col = np.arange(TOK), np.arange(BAND)
    near_row = np.abs(tok[:, None] // W + 1 - col[None, :] // W) <= 1
    near_col = np.abs(tok[:, None] % W - col[None, :] % W) <= 1
    per_channel = {
        "dw_b": L1_conv_dw_b, "pw_b": L1_conv_pw_b, "b_ln": L2_conv_bln, "b_v": np.asarray(L2_conv_bqkv)[2 * C:],
        "bn1_g": L1_conv_bn1_g, "bn1_b": L1_conv_bn1_b, "bn1_m": L1_conv_bn1_m, "bn1_v": L1_conv_bn1_v,
        "bn2_g": L1_conv_bn2_g, "bn2_b": L1_conv_bn2_b, "bn2_m": L1_conv_bn2_m, "bn2_v": L1_conv_bn2_v,
    }
    arrays = {
        "x": x,
        "gate_wT": np.asarray(L0_conv_gate_w).T,
        "gate_b": L0_conv_gate_b,
        "expert_wT": np.asarray(L0_conv_expert_w).transpose(0, 2, 1),
        "dw_w": L1_conv_dw_w,
        "channel_params": np.stack([np.asarray(per_channel[name]).reshape(J, P) for name in PARAMS]).transpose(2, 0, 1),
        "pw_wT": np.asarray(L1_conv_pw_w)[:, :, 0, 0].T,
        "w_qk": np.asarray(L2_conv_Wqkv)[:, :2 * C],
        "b_qk": np.asarray(L2_conv_bqkv)[:2 * C],
        "w_vT": np.asarray(L2_conv_Wqkv)[:, 2 * C:].T,
        "w_ln": L2_conv_Wln,
        "group_mean": group_mean,
        "ident": np.eye(P, dtype=np.float32),
        "box_band": (near_row & near_col).astype(np.float32),
    }
    arrays = {name: np.ascontiguousarray(a) for name, a in arrays.items()}
    nc = bacc.Bacc("TRN2", target_bir_lowering=False, num_devices=1)
    t = {name: nc.dram_tensor(name, a.shape, mybir.dt.from_np(a.dtype), kind="ExternalInput").ap()
         for name, a in arrays.items()}
    out = nc.dram_tensor("out", (IMAGES, C, H, W), F32, kind="ExternalOutput").ap()
    build(nc, out=out, **t)
    r = run_bass_kernel_spmd(nc, [arrays], core_ids=[0])
    return r.results[0]["out"]
```

```python
from contextlib import ExitStack

import concourse.bass as bass
from concourse import mybir

ALU = mybir.AluOpType
ACT = mybir.ActivationFunctionType
F32 = mybir.dt.float32
F32R = mybir.dt.float32r
BF16 = mybir.dt.bfloat16
AX = mybir.AxisListType

P = 128
IMAGES = 32
C = 256
J = C // P
H = W = 28
HW = H * W
HALF = HW // 2
EXPERTS = 8
GROUP = C // 32
TAPS = 9
PH, PW = H + 2, W + 2
TOK = 112
M = HW // TOK
BOX_STEPS = 4
MIX_SLOTS = 4
UNROLL = 2
STAGES = 7
PARAMS = ["dw_b", "pw_b", "b_ln", "b_v", "bn1_g", "bn1_b", "bn1_m", "bn1_v", "bn2_g", "bn2_b", "bn2_m", "bn2_v"]

GN_EPS = 1e-5
BN_EPS = 1e-5
DW_THRESH = 4.0
PW_THRESH = 0.001
DIV_EPS = 1e-7
NORM_EPS = 1e-12

GN_SQ, GN_VAR, GN_R, GN_DONE = 1, 2, 3, 4


class Image:

    def __init__(self, pair, offset):
        self.pair, self.offset = pair, offset

    def __sub__(self, n):
        return Image(self.pair, self.offset - n)

    def __add__(self, n):
        return Image(self.pair, self.offset + n)

    def times(self, per, more=0):
        if self.pair is None:
            return per * self.offset + more
        return self.pair * (per * UNROLL) + (per * self.offset + more)

    @property
    def odd(self):
        return self.offset % 2

    @property
    def active(self):
        return self.pair is not None or 0 <= self.offset < IMAGES

    @property
    def first(self):
        return self.pair is None and self.offset == 0

    @property
    def started(self):
        return self.pair is not None or self.offset >= 0


class Count:

    def __init__(self, sem, per=1):
        self.sem, self.per = sem, per

    def at(self, image, count=None):
        return image.times(self.per, self.per if count is None else count)


class DmaCount:

    def __init__(self, sems):
        self.sems = sems

    def of(self, image):
        return self.sems[image.odd]

    def at(self, image):
        turn = 16 * (image.offset // 2 + 1)
        return turn if image.pair is None else image.pair * 16 + turn


def build(nc, x, gate_wT, gate_b, expert_wT, dw_w, channel_params, pw_wT, w_qk, b_qk, w_vT, w_ln, group_mean, ident, out):
    with ExitStack() as ctx:
        def sb(name, shape, dt=F32):
            return ctx.enter_context(nc.sbuf_tensor(name, shape, dt))

        def sem(name):
            return ctx.enter_context(nc.semaphore(name))

        def sig(name, per=1):
            return Count(sem(name), per)

        gate_w_sb = sb("gate_w_sb", [P, J, EXPERTS])
        gate_b_sb = sb("gate_b_sb", [P, EXPERTS])
        expert_sb = sb("expert_sb", [P, EXPERTS, J * C])
        dw_sb = sb("dw_sb", [P, J, TAPS])
        params = sb("params", [P, len(PARAMS), J])
        dwb_sb, pwb_sb, bln_sb, bv_col = (params[:, n, :] for n in range(4))
        bn1_sb, bn2_sb = params[:, 4:8, :], params[:, 8:12, :]
        pw_sb = sb("pw_sb", [P, J, C])
        wqk = sb("wqk", [P, 2, J, 2 * C], F32R)
        w_out = sb("w_out", [P, 2, J, C], F32R)
        gmean = sb("gmean", [P, P])
        idn = sb("idn", [P, P])
        ones = sb("ones", [P, P])
        ones3 = sb("ones3", [3, TOK], BF16)
        bqk3 = sb("bqk3", [3, 2 * C], BF16)
        bn_scale = sb("bn_scale", [P, 2, J])
        bn_shift = sb("bn_shift", [P, 2, J])
        bn_tmp = sb("bn_tmp", [P, 2, J])
        qk_mean = sb("qk_mean", [P, J, 2])
        bqk_mean = sb("bqk_mean", [1, 2])
        b_out = sb("b_out", [P, J])
        bv_ln = sb("bv_ln", [1, C])

        x0 = sb("x0", [P, 2, J, HW])
        xn0 = sb("xn0", [P, J, HW])
        mixed = sb("mixed", [P, J * C])
        mix_tmp = sb("mix_tmp", [P, MIX_SLOTS, J * C])
        x1 = sb("x1", [P, 2, J, HW])
        xpad = sb("xpad", [P, J, PH, PW])
        h = sb("h", [P, 2, J, HW])
        pw_masked = sb("pw_masked", [P, J, C])
        x2 = sb("x2", [P, 2, J, HW])
        xn2 = sb("xn2", [P, J, HW])
        xn2_parts = sb("xn2_parts", [P, 2, J, HW], F32R)
        q2 = sb("q2", [TOK, M, C])
        k2 = sb("k2", [TOK, M, C])
        junk = sb("junk", [P, M * C], BF16)
        ksq = sb("ksq", [TOK, 2, C])
        ksum = sb("ksum", [TOK, 2, C])
        xT = sb("xT", [TOK, M, C])
        kx_parts = sb("kx_parts", [P, 2, J, C], F32R)
        attn_parts = sb("attn_parts", [P, 2, J, C], F32R)
        qT_parts = sb("qT_parts", [P, 2, J, HW], F32R)
        x3 = sb("x3", [P, 2, J, HW])
        x3pad = sb("x3pad", [P, J, PH, PW])
        row_sums = sb("row_sums", [P, J, PH, W])

        wqk_raw = x3[:, 0].rearrange("p j n -> p (j n)")[:, 0:J * 2 * C].rearrange("p (j n) -> p j n", j=J)
        wv_ln = x3[:, 1].rearrange("p j n -> p (j n)")[:, 0:2 * J * C].rearrange("p (w j n) -> p w j n", w=2, j=J)
        wvT_sb, wln_sb = wv_ln[:, 0], wv_ln[:, 1]
        bias_rows = xn2[0:1].rearrange("p j n -> p (j n)")[:, 0:3 * 2 * C].rearrange("p (k n) -> p k n", k=3)
        bqk_row, bqk_rest = bias_rows[:, 0, :], bias_rows[:, 1:3, :]
        bqk_parts = xT[0:1].rearrange("p m c -> p (m c)")[:, 0:3 * C].bitcast(BF16).rearrange("p (k n) -> p k n", k=3)

        gn_in = sb("gn_in", [P, 4, 4])
        gn_avg = sb("gn_avg", [P, 4, 4])
        gn_sq = sb("gn_sq", [P, 4, J])
        gn_var = sb("gn_var", [P, 4, J])
        gn_sd = sb("gn_sd", [P, 4, J])
        gn_r = sb("gn_r", [P, 4, J])
        gn_s = sb("gn_s", [P, 4, J])
        pooled = sb("pooled", [P, 2, J])
        gate_in = sb("gate_in", [P, J, EXPERTS])
        z = sb("z", [P, EXPERTS])
        zz = sb("zz", [P, 2, EXPERTS, EXPERTS])
        excess = sb("excess", [P, EXPERTS])
        support = sb("support", [P, 2, EXPERTS])
        tau = sb("tau", [P, 4])
        gate = sb("gate", [P, EXPERTS])
        hmax = sb("hmax", [P, J])
        hmask = sb("hmask", [P, J])
        ymax = sb("ymax", [P, J])
        ymask = sb("ymask", [P, J])
        qk_sum = sb("qk_sum", [TOK, 2, M])
        qk_rec = sb("qk_rec", [TOK, 2, M])
        q_nsq = sb("q_nsq", [TOK, M])
        q_norm = sb("q_norm", [TOK, M])
        q_alpha = sb("q_alpha", [TOK, 3, M])
        k_norm = sb("k_norm", [P, J])
        k_inv = sb("k_inv", [P, 2, J])
        k_row = sb("k_row", [1, C])

        conv_ps = ctx.enter_context(nc.psum_tensor("conv_ps", [P, 4, 512], F32))
        tile_ps = ctx.enter_context(nc.psum_tensor("tile_ps", [P, 3, 512], F32))
        small_ps = ctx.enter_context(nc.psum_tensor("small_ps", [P, 512], F32))

        held = {name: sem(f"held_{name}") for name in ("dve", "pool", "sp")}

        def hold(eng, name):
            eng.sem_inc(held[name], 1)

        gate_loaded = sem("gate_loaded")
        w_loaded = sem("w_loaded")
        experts_loaded = sem("experts_loaded")
        setup_dve = sem("setup_dve")
        setup_act = sem("setup_act")
        setup_pe = sem("setup_pe")
        setup_pool = sem("setup_pool")
        bias_moved = sem("bias_moved")
        x_loaded = DmaCount([sem("x_loaded_even"), sem("x_loaded_odd")])
        stored = DmaCount([sem("stored_even"), sem("stored_odd")])
        gn = sig("gn", GN_DONE)
        gn_sums = [sig(f"gn_sums{n}", 2 * J if n == 0 else J) for n in range(4)]
        gn_mm = sig("gn_mm")
        gn_read = sig("gn_read")
        gn_sqrt = sig("gn_sqrt")
        xn0_ready = sig("xn0_ready", J)
        gate_step = sig("gate_step", 14)
        gate_mm = sig("gate_mm")
        mix_mul = sig("mix_mul", 1 + MIX_SLOTS)
        mix_mul_rest = sig("mix_mul_rest", EXPERTS - 1 - MIX_SLOTS)
        mix_step = sig("mix_step", EXPERTS - 1)
        conv0_mm = sig("conv0_mm", J)
        x1_ready = sig("x1_ready", J)
        xpad_ready = sig("xpad_ready", J)
        dw_step = [sig(f"dw_step{j}", TAPS) for j in range(J)]
        h_ready = sig("h_ready", J)
        hmask_step = sig("hmask_step", 2)
        pw_masked_ready = sig("pw_masked_ready", J)
        pw_mm = sig("pw_mm", J)
        y_ready = sig("y_ready", J)
        ymask_step = sig("ymask_step", 2)
        x2_ready = sig("x2_ready", J)
        xn2_ready = sig("xn2_ready", J)
        xn2_hi = sig("xn2_hi", J)
        xn2_lo = sig("xn2_lo", J)
        qk_mm = sig("qk_mm", M)
        q2_ready = sig("q2_ready", M)
        k2_ready = sig("k2_ready", M)
        rec_step = sig("rec_step", 2)
        kn_ready = sig("kn_ready", M)
        q4_ready = sig("q4_ready", M)
        q_root = sig("q_root")
        alpha_step = sig("alpha_step", 3)
        qa_ready = sig("qa_ready", M)
        ksum_step = sig("ksum_step", 3 * M - 2)
        xT_mm = sig("xT_mm", 4)
        xT_ready = sig("xT_ready", 4)
        kx_mm = sig("kx_mm")
        kx_hi = sig("kx_hi")
        kx_lo = sig("kx_lo")
        ksum_mm = sig("ksum_mm")
        ksum_read = sig("ksum_read", 2)
        kinv_step = sig("kinv_step", 2)
        attn_w_mm = sig("attn_w_mm")
        attn_hi = sig("attn_hi", J)
        attn_lo = sig("attn_lo", J)
        qT_mm = sig("qT_mm", 4)
        qT_hi = sig("qT_hi", 4)
        qT_lo = sig("qT_lo", 4)
        value_mm = sig("value_mm", J)
        attn_mm = sig("attn_mm", J)
        x3_ready = sig("x3_ready", J)
        x3pad_ready = sig("x3pad_ready", J)
        box_step = [sig(f"box_step{j}", BOX_STEPS) for j in range(J)]
        x4_ready = sig("x4_ready", J)

        x_dram = x.rearrange("b (j p) h w -> b p j (h w)", p=P)
        out_dram = out.rearrange("b (j p) h w -> b p j (h w)", p=P)

        def half(j):
            return slice(j * P, (j + 1) * P)

        def split(tile):
            return tile.rearrange("p (a n) -> p a n", a=2)

        def box_operands(j, n):
            inner = x3pad[:, j, 1:1 + H, 1:1 + W]
            sums = row_sums[:, j, 1:1 + H, :]
            return [(sums, x3pad[:, j, 1:1 + H, 0:W], inner),
                    (sums, sums, x3pad[:, j, 1:1 + H, 2:2 + W]),
                    (inner, row_sums[:, j, 0:H, :], sums),
                    (inner, inner, row_sums[:, j, 2:2 + H, :])][n]

        def conv_banks(j):
            return conv_ps[:, 2 * j:2 * j + 2, 0:HALF]

        def run(eng, step):
            first, last = 8, IMAGES - 2
            for t in range(-1, first):
                step(Image(None, t))
            with eng.Fori(first // UNROLL, last // UNROLL) as pair:
                for u in range(UNROLL):
                    step(Image(pair, u))
            for t in range(last, IMAGES + STAGES - 2):
                step(Image(None, t))

        PAIRS = [[2 * b, 2 * b + 1] if 2 * b + 1 < M else [2 * b] for b in range(4)]
        QUADS = [(j, ms) for j in range(J) for ms in ([0, 1, 2, 3], [4, 5, 6])]
        TAP_TURNS = [(0, 0)] + [turn for n in range(1, TAPS) for turn in ((0, n), (1, n - 1))] + [(1, TAPS - 1)]

        block = ctx.enter_context(nc.Block())

        gate_loads = [
            (gmean[:], group_mean),
            (gate_w_sb[:], gate_wT.rearrange("(j p) k -> p j k", p=P)),
            (gate_b_sb[:], gate_b[None, :].to_broadcast([P, EXPERTS])),
        ]
        loads = [
            (params[:], channel_params),
            (bqk_row, b_qk[None, :]),
            (wqk_raw, w_qk.rearrange("(j p) o -> p j o", p=P)),
            (wvT_sb, w_vT.rearrange("(j p) o -> p j o", p=P)),
            (wln_sb, w_ln.rearrange("(j p) o -> p j o", p=P)),
            (dw_sb[:], dw_w.rearrange("(j p) a b c -> p j (a b c)", p=P)),
            (idn[:], ident),
            (pw_sb[:], pw_wT.rearrange("(j p) o -> p j o", p=P)),
        ]
        GATE_LOADED, LOADED, EXPERTS_LOADED = 16 * len(gate_loads), 16 * len(loads), 16 * EXPERTS

        @block.sync
        def _(sp):
            sp.dma_start(x0[:, 0], x_dram[0]).then_inc(x_loaded.sems[0], 16)
            for dst, src in gate_loads:
                sp.dma_start(dst, src).then_inc(gate_loaded, 16)
            for dst, src in loads:
                sp.dma_start(dst, src).then_inc(w_loaded, 16)
            for k in range(EXPERTS):
                sp.dma_start(expert_sb[:, k, :].rearrange("p (j o) -> p j o", j=J),
                             expert_wT[k].rearrange("(j p) o -> p j o", p=P)).then_inc(experts_loaded, 16)

            def step(t):
                Z, F = t + 1, t - 5
                if Z.active and (Z.pair is not None or Z.offset > 0):
                    if (Z - 2).active:
                        sp.wait_ge(x1_ready.sem, x1_ready.at(Z - 2))
                        hold(sp, "sp")
                    sp.dma_start(x0[:, Z.odd], x_dram[Z.times(1)]).then_inc(x_loaded.of(Z), 16)
                if F.active:
                    sp.wait_ge(x4_ready.sem, x4_ready.at(F))
                    sp.dma_start(out_dram[F.times(1)], x3[:, F.odd]).then_inc(stored.of(F), 16)

            run(sp, step)
            for last in (Image(None, IMAGES - 2), Image(None, IMAGES - 1)):
                sp.wait_ge(stored.of(last), stored.at(last))

        @block.tensor
        def _(pe):
            def setup():
                pe.wait_ge(w_loaded, LOADED)
                for i in range(J):
                    for d in range(J):
                        mm = nc.tensor.matmul(tile_ps[:, 0, i * C:(i + 1) * C], wvT_sb[:, d, half(i)],
                                              wln_sb[:, d, :], start=(d == 0), stop=(d == J - 1))
                mm.then_inc(setup_pe, 1)
                for o in range(J):
                    for d in range(J):
                        mm = nc.tensor.matmul(tile_ps[:, 1, o:o + 1], wln_sb[:, d, half(o)], bv_col[:, d:d + 1],
                                              start=(d == 0), stop=(d == J - 1))
                for d in range(J):
                    mm = nc.tensor.matmul(tile_ps[0:1, 2, 0:C], bv_col[:, d:d + 1], wln_sb[:, d, :],
                                          start=(d == 0), stop=(d == J - 1))
                mm.then_inc(setup_pe, 1)

            def setup_done():
                pe.wait_ge(setup_dve, SETUP_DVE)
                pe.wait_ge(bias_moved, 48)

            pe.wait_ge(gate_loaded, GATE_LOADED)
            pe.wait_ge(setup_pool, SETUP_POOL)

            def wait_free(*readers):
                for img, count, k in readers:
                    if img.active:
                        pe.wait_ge(count.sem, count.at(img, k))
                        return

            def group_means(Z, A, C_, E):
                if A.active:
                    pe.wait_ge(gate_step.sem, gate_step.at(A, 4))
                elif A.started:
                    pe.wait_ge(gn_read.sem, gn_read.at(A))
                if Z.active:
                    pe.wait_ge(gn_sums[0].sem, gn_sums[0].at(Z))
                for img, layer, made in ((A, 1, x1_ready), (C_, 2, x2_ready), (E, 3, x3_ready)):
                    if img.active:
                        pe.wait_ge(made.sem, made.at(img))
                        pe.wait_ge(gn_sums[layer].sem, gn_sums[layer].at(img))
                nc.tensor.matmul(small_ps[:, 0:16], gmean[:], gn_in[:].rearrange("p l n -> p (l n)"), start=True,
                                 stop=True).then_inc(gn_mm.sem, 1)

            def gate_logits(A):
                pe.wait_ge(gn_read.sem, gn_read.at(A))
                pe.wait_ge(gate_step.sem, gate_step.at(A, 3))
                for j in range(J):
                    mm = nc.tensor.matmul(small_ps[:, 0:EXPERTS], ones[:], gate_in[:, j, :], start=(j == 0),
                                          stop=(j == J - 1))
                mm.then_inc(gate_mm.sem, 1)

            def conv_tile(j, parts, first=True, last=True):
                for i, (wt, act) in enumerate(parts):
                    for a in range(2):
                        mm = nc.tensor.matmul(conv_ps[:, 2 * j + a, 0:HALF], wt[:, half(j)],
                                              act[:, a * HALF:(a + 1) * HALF],
                                              start=(first and i == 0), stop=(last and i == len(parts) - 1),
                                              skip_group_check=True)
                return mm

            def by_parts(wt, act):
                return [(wt[:, u, i, :], act[:, v, i, :]) for i in range(J) for u, v in ((0, 0), (0, 1), (1, 0))]

            def q_to_channels(E, banks):
                pe.wait_ge(qa_ready.sem, qa_ready.at(E))
                before = [[], [], [(E, kx_lo, 1)], [(E, qT_lo, 1)]]
                for n in banks:
                    j, ms = QUADS[n]
                    wait_free(*before[n])
                    for s, m in enumerate(ms):
                        mm = nc.tensor.transpose(tile_ps[:, QT_BANK[n], s * TOK:(s + 1) * TOK], q2[:, m, half(j)],
                                                 idn[0:TOK, 0:TOK])
                    mm.then_inc(qT_mm.sem, 1)

            def to_tokens(b, bank, source):
                for s, m in enumerate(PAIRS[b]):
                    for i in range(J):
                        mm = nc.tensor.transpose(tile_ps[0:TOK, bank, s * C + i * P:s * C + (i + 1) * P],
                                                 source[:, i, m * TOK:(m + 1) * TOK], idn[:])
                return mm

            def key_sums(E):
                wait_free((E, qT_lo, 2))
                pe.wait_ge(ksum_step.sem, ksum_step.at(E))
                bank = tile_ps[:, KSUM_BANK, :]
                nc.tensor.matmul(bank[0:1, 0:C], ones[0:TOK, 0:1], ksum[:, 0, :], start=True, stop=True)
                for c in range(J):
                    mm = nc.tensor.matmul(bank[:, C + c:C + c + 1], ksum[:, 1, half(c)], ones[0:TOK, 0:1],
                                          start=True, stop=True)
                mm.then_inc(ksum_mm.sem, 1)

            def attention_weights(E):
                wait_free((E, qT_lo, 3))
                pe.wait_ge(kx_lo.sem, kx_lo.at(E))
                pe.wait_ge(ksum_read.sem, ksum_read.at(E))
                for c in range(J):
                    dst = tile_ps[:, ATTN_BANK, c * C:(c + 1) * C]
                    nc.tensor.matmul(dst, k_row[:, half(c)], bv_ln[:], start=True, stop=False)
                    for i in range(J):
                        for u, v in ((0, 0), (0, 1), (1, 0)):
                            mm = nc.tensor.matmul(dst, kx_parts[:, u, i, half(c)], w_out[:, v, i, :], start=False,
                                                  stop=(i == J - 1 and u == 1))
                mm.then_inc(attn_w_mm.sem, 1)

            def value_out(B, D, E, F, j):
                wait_free((B, x1_ready, j + 1), (D, y_ready, j + 1), (F, x3_ready, j + 1))
                conv_tile(j, by_parts(w_out, xn2_parts), last=False).then_inc(value_mm.sem, 1)

            def attention_out(E, j):
                pe.wait_ge(attn_lo.sem, attn_lo.at(E))
                pe.wait_ge(qT_lo.sem, qT_lo.at(E))
                conv_tile(j, by_parts(attn_parts, qT_parts), first=False).then_inc(attn_mm.sem, 1)

            def pointwise(C_):
                pe.wait_ge(h_ready.sem, h_ready.at(C_))
                pe.wait_ge(pw_masked_ready.sem, pw_masked_ready.at(C_))
                for j in range(J):
                    wait_free((C_ - 2, x3_ready, j + 1), (C_ + 1, x1_ready, j + 1))
                    conv_tile(j, [(pw_masked[:, i, :], h[:, C_.odd, i, :]) for i in range(J)]).then_inc(pw_mm.sem, 1)

            def queries_keys(D):
                pe.wait_ge(xn2_lo.sem, xn2_lo.at(D))
                before = [[(D - 1, attn_lo, J)], [(D, xT_ready, 3)], [(D, xT_ready, 4)]
                          ] + [[(D, k2_ready, m - 2)] for m in range(3, M)]
                for m in range(M):
                    wait_free(*before[m])
                    bank = tile_ps[0:TOK, QK_BANK[m], :]
                    nc.tensor.matmul(bank, ones3[:], bqk3[:], start=True, stop=False)
                    for i in range(J):
                        for u, v in ((0, 0), (0, 1), (1, 0)):
                            mm = nc.tensor.matmul(bank, xn2_parts[:, u, i, m * TOK:(m + 1) * TOK], wqk[:, v, i, :],
                                                  start=False, stop=(i == J - 1 and u == 1))
                    mm.then_inc(qk_mm.sem, 1)

            def x2_to_tokens(D, E, banks):
                pe.wait_ge(xn2_ready.sem, xn2_ready.at(D))
                before = [[(E, qT_lo, 4)], [(E, ksum_read, 2)], [(D, xT_ready, 1)], [(D, xT_ready, 2)]]
                for b in banks:
                    wait_free(*before[b])
                    to_tokens(b, XT_BANK[b], xn2).then_inc(xT_mm.sem, 1)

            def mixed_conv(A):
                pe.wait_ge(xn0_ready.sem, xn0_ready.at(A))
                pe.wait_ge(mix_step.sem, mix_step.at(A))
                for j in range(J):
                    wait_free((A - 2, y_ready, j + 1), (A - 1, x1_ready, j + 1))
                    conv_tile(j, [(mixed[:, i * C:(i + 1) * C], xn0[:, i, :]) for i in range(J)]
                              ).then_inc(conv0_mm.sem, 1)

            def keys_x(D):
                pe.wait_ge(kn_ready.sem, kn_ready.at(D))
                pe.wait_ge(xT_ready.sem, xT_ready.at(D))
                for i in range(J):
                    for m in range(M):
                        mm = nc.tensor.matmul(tile_ps[:, KX_BANK, i * C:(i + 1) * C], xT[:, m, half(i)], k2[:, m, :],
                                              start=(m == 0), stop=(m == M - 1))
                mm.then_inc(kx_mm.sem, 1)

            def step(t):
                Z, A, B, C_, D, E, F = (t + 1 - n for n in range(STAGES))
                if E.active:
                    for j in range(J):
                        value_out(B, D, E, F, j)
                    q_to_channels(E, range(3))
                if A.active:
                    gate_logits(A)
                if t.first:
                    setup()
                if E.active:
                    q_to_channels(E, range(3, 4))
                    key_sums(E)
                if D.active:
                    x2_to_tokens(D, E, range(1))
                if E.active:
                    attention_weights(E)
                if D.active:
                    x2_to_tokens(D, E, range(1, 3))
                if E.active:
                    attention_out(E, 0)
                if D.active:
                    x2_to_tokens(D, E, range(3, 4))
                if E.active:
                    attention_out(E, 1)
                if D.active:
                    queries_keys(D)
                if C_.active:
                    pointwise(C_)
                if A.active:
                    mixed_conv(A)
                if t.first:
                    setup_done()
                if D.active:
                    keys_x(D)
                if t.pair is not None or t.offset < IMAGES + STAGES - 3:
                    group_means(Z, A, C_, E)

            run(pe, step)

        @block.vector
        def _(dve):
            setup = [0]

            def did(ins):
                ins.then_inc(setup_dve, 1)
                setup[0] += 1
                dve.wait_ge(setup_dve, setup[0])

            def parts_of(dst, source):
                did(nc.vector.tensor_copy(dst[:, 0], source))
                did(nc.vector.tensor_tensor(dst[:, 1], source, dst[:, 0].bitcast(F32), ALU.subtract))

            dve.wait_ge(gate_loaded, GATE_LOADED)

            def setup_weights():
                dve.wait_ge(w_loaded, LOADED)
                for j in range(J):
                    for s in range(2):
                        cols = slice(s * C, (s + 1) * C)
                        did(nc.vector.tensor_reduce(qk_mean[:, j, s:s + 1], wqk_raw[:, j, cols], AX.X, ALU.add))
                        did(nc.vector.tensor_scalar(qk_mean[:, j, s:s + 1], qk_mean[:, j, s:s + 1], 1.0 / C, None, ALU.mult))
                        did(nc.vector.tensor_scalar(wqk_raw[:, j, cols], wqk_raw[:, j, cols], qk_mean[:, j, s:s + 1], None,
                                                    ALU.subtract))
                for s in range(2):
                    cols = slice(s * C, (s + 1) * C)
                    did(nc.vector.tensor_reduce(bqk_mean[:, s:s + 1], bqk_row[:, cols], AX.X, ALU.add))
                    did(nc.vector.tensor_scalar(bqk_mean[:, s:s + 1], bqk_mean[:, s:s + 1], 1.0 / C, None, ALU.mult))
                    did(nc.vector.tensor_scalar(bqk_row[:, cols], bqk_row[:, cols], bqk_mean[:, s:s + 1], None,
                                                ALU.subtract))
                did(nc.vector.tensor_copy(bqk_parts[:, 0, :], bqk_row))
                did(nc.vector.tensor_tensor(bqk_rest[:, 0, :], bqk_row, bqk_parts[:, 0, :], ALU.subtract))
                did(nc.vector.tensor_copy(bqk_parts[:, 1, :], bqk_rest[:, 0, :]))
                did(nc.vector.tensor_tensor(bqk_rest[:, 1, :], bqk_rest[:, 0, :], bqk_parts[:, 1, :], ALU.subtract))
                did(nc.vector.tensor_copy(bqk_parts[:, 2, :], bqk_rest[:, 1, :]))
                for n, (bn, bias) in enumerate(((bn1_sb, dwb_sb), (bn2_sb, pwb_sb))):
                    did(nc.vector.tensor_scalar(bn_tmp[:, n, :], bn[:, 3, :], BN_EPS, None, ALU.add))
                dve.wait_ge(setup_act, 1)
                for n, (bn, bias) in enumerate(((bn1_sb, dwb_sb), (bn2_sb, pwb_sb))):
                    did(nc.vector.reciprocal(bn_scale[:, n, :], bn_shift[:, n, :]))
                    did(nc.vector.tensor_tensor(bn_scale[:, n, :], bn_scale[:, n, :], bn[:, 0, :], ALU.mult))
                    did(nc.vector.tensor_tensor(bn_tmp[:, n, :], bias, bn[:, 2, :], ALU.subtract))
                    did(nc.vector.tensor_tensor(bn_tmp[:, n, :], bn_tmp[:, n, :], bn_scale[:, n, :], ALU.mult))
                    did(nc.vector.tensor_tensor(bn_shift[:, n, :], bn_tmp[:, n, :], bn[:, 1, :], ALU.add))
                parts_of(wqk, wqk_raw)
                dve.wait_ge(setup_pe, 2)
                parts_of(w_out, tile_ps[:, 0, :].rearrange("p (i c) -> p i c", i=J))
                did(nc.vector.tensor_tensor(b_out[:], tile_ps[:, 1, 0:J], bln_sb, ALU.add))
                did(nc.vector.tensor_copy(bv_ln[:], tile_ps[0:1, 2, 0:C]))
                assert setup[0] == SETUP_DVE

            def variances(A):
                dve.wait_ge(gn_mm.sem, gn_mm.at(A))
                nc.vector.tensor_copy(gn_avg[:].rearrange("p l n -> p (l n)"), small_ps[:, 0:16]
                                      ).then_inc(gn_read.sem, 1)
                dve.wait_ge(gn_read.sem, gn_read.at(A))
                mean, mean_sq = gn_avg[:, :, 0:2], gn_avg[:, :, 2:4]
                nc.vector.tensor_tensor(gn_sq[:], mean, mean, ALU.mult).then_inc(gn.sem, 1)
                dve.wait_ge(gn.sem, gn.at(A, GN_SQ))
                nc.vector.scalar_tensor_tensor(gn_var[:], mean_sq, GN_EPS, gn_sq[:], ALU.add,
                                               ALU.subtract).then_inc(gn.sem, 1)

            def scales_shifts(A):
                dve.wait_ge(gn_sqrt.sem, gn_sqrt.at(A))
                nc.vector.reciprocal(gn_r[:], gn_sd[:]).then_inc(gn.sem, 1)
                dve.wait_ge(gn.sem, gn.at(A, GN_R))
                nc.vector.scalar_tensor_tensor(gn_s[:], gn_avg[:, :, 0:2], -1.0, gn_r[:], ALU.mult,
                                               ALU.mult).then_inc(gn.sem, 1)

            def gate_logits(A):
                s = gate_step
                dve.wait_ge(gn.sem, gn.at(A))
                nc.vector.scalar_tensor_tensor(pooled[:, 0, :], gn_in[:, 0, 0:2], 1.0 / HW, gn_r[:, 0, :], ALU.mult,
                                               ALU.mult).then_inc(s.sem, 1)
                dve.wait_ge(s.sem, s.at(A, 1))
                nc.vector.tensor_tensor(pooled[:, 1, :], pooled[:, 0, :], gn_s[:, 0, :], ALU.add).then_inc(s.sem, 1)
                dve.wait_ge(s.sem, s.at(A, 2))
                nc.vector.tensor_tensor(gate_in[:], gate_w_sb[:],
                                        pooled[:, 1, :].unsqueeze(2).to_broadcast([P, J, EXPERTS]),
                                        ALU.mult).then_inc(s.sem, 1)

            def sparsemax(A):
                s = gate_step
                dve.wait_ge(gate_mm.sem, gate_mm.at(A))
                nc.vector.tensor_tensor(z[:], small_ps[:, 0:EXPERTS], gate_b_sb[:], ALU.add).then_inc(s.sem, 1)
                dve.wait_ge(s.sem, s.at(A, 4))
                nc.vector.tensor_tensor(zz[:, 0], z[:].unsqueeze(1).to_broadcast([P, EXPERTS, EXPERTS]),
                                        z[:].unsqueeze(2).to_broadcast([P, EXPERTS, EXPERTS]),
                                        ALU.subtract).then_inc(s.sem, 1)
                dve.wait_ge(s.sem, s.at(A, 5))
                nc.vector.tensor_scalar(zz[:, 1], zz[:, 0], 0.0, None, ALU.max).then_inc(s.sem, 1)
                dve.wait_ge(s.sem, s.at(A, 6))
                nc.vector.tensor_reduce(excess[:], zz[:, 1], AX.X, ALU.add).then_inc(s.sem, 1)
                dve.wait_ge(s.sem, s.at(A, 7))
                nc.vector.tensor_scalar(support[:, 0, :], excess[:], 1.0, None, ALU.is_lt).then_inc(s.sem, 1)
                dve.wait_ge(s.sem, s.at(A, 8))
                nc.vector.tensor_tensor(support[:, 1, :], support[:, 0, :], z[:], ALU.mult).then_inc(s.sem, 1)
                dve.wait_ge(s.sem, s.at(A, 9))
                nc.vector.tensor_reduce(tau[:, 0:2], support[:], AX.X, ALU.add).then_inc(s.sem, 1)
                dve.wait_ge(s.sem, s.at(A, 10))
                nc.vector.reciprocal(tau[:, 2:3], tau[:, 0:1]).then_inc(s.sem, 1)
                nc.vector.tensor_scalar(tau[:, 1:2], tau[:, 1:2], -1.0, None, ALU.add).then_inc(s.sem, 1)
                dve.wait_ge(s.sem, s.at(A, 12))
                nc.vector.tensor_tensor(tau[:, 3:4], tau[:, 1:2], tau[:, 2:3], ALU.mult).then_inc(s.sem, 1)
                dve.wait_ge(s.sem, s.at(A, 13))
                if (A - 1).active:
                    dve.wait_ge(mix_step.sem, mix_step.at(A - 1))
                nc.vector.tensor_scalar(gate[:], z[:], tau[:, 3:4], 0.0, ALU.subtract, ALU.max).then_inc(s.sem, 1)

            def depthwise(B, turns):
                for j, tap in TAP_TURNS[turns]:
                    if tap == 0:
                        dve.wait_ge(xpad_ready.sem, xpad_ready.at(B, j + 1))
                        if (B - 2).active:
                            dve.wait_ge(pw_mm.sem, pw_mm.at(B - 2))
                    acc = h[:, B.odd, j, :].rearrange("p (h w) -> p h w", w=W)
                    view = xpad[:, j, tap // 3:tap // 3 + H, tap % 3:tap % 3 + W]
                    scalar = dw_sb[:, j, tap:tap + 1]
                    if tap == 0:
                        dve.wait_ge(w_loaded, LOADED)
                        ins = nc.vector.tensor_scalar(acc, view, scalar, None, ALU.mult)
                    else:
                        dve.wait_ge(dw_step[j].sem, dw_step[j].at(B, tap))
                        ins = nc.vector.scalar_tensor_tensor(acc, view, scalar, acc, ALU.mult, ALU.add)
                    ins.then_inc(dw_step[j].sem, 1)

            def h_mask(C_):
                dve.wait_ge(h_ready.sem, h_ready.at(C_))
                nc.vector.tensor_reduce(hmax[:], h[:, C_.odd], AX.X, ALU.max).then_inc(hmask_step.sem, 1)
                dve.wait_ge(hmask_step.sem, hmask_step.at(C_, 1))
                if (C_ - 1).active:
                    dve.wait_ge(pw_masked_ready.sem, pw_masked_ready.at(C_ - 1))
                nc.vector.tensor_scalar(hmask[:], hmax[:], DW_THRESH, None, ALU.is_ge).then_inc(hmask_step.sem, 1)

            def make_x2(C_):
                dve.wait_ge(y_ready.sem, y_ready.at(C_))
                nc.vector.tensor_reduce(ymax[:], x2[:, C_.odd], AX.X, ALU.max).then_inc(ymask_step.sem, 1)
                dve.wait_ge(ymask_step.sem, ymask_step.at(C_, 1))
                nc.vector.tensor_scalar(ymask[:], ymax[:], PW_THRESH, None, ALU.is_ge).then_inc(ymask_step.sem, 1)
                dve.wait_ge(ymask_step.sem, ymask_step.at(C_, 2))
                for j in range(J):
                    y = x2[:, C_.odd, j, :]
                    nc.vector.scalar_tensor_tensor(y, y, ymask[:, j:j + 1], x1[:, C_.odd, j, :], ALU.mult, ALU.add,
                                                   accum_out=gn_in[:, 2, j:j + 1]).then_inc(x2_ready.sem, 1)

            def make_x1(A):
                if (A - 2).active:
                    dve.wait_ge(x2_ready.sem, x2_ready.at(A - 2))
                for j in range(J):
                    dve.wait_ge(conv0_mm.sem, conv0_mm.at(A, j + 1))
                    nc.vector.scalar_tensor_tensor(split(x1[:, A.odd, j, :]), conv_banks(j), 1.0,
                                                   split(x0[:, A.odd, j, :]), ALU.mult, ALU.add,
                                                   accum_out=gn_in[:, 1, j:j + 1]).then_inc(x1_ready.sem, 1)

            def make_x3(E):
                if (E - 2).active:
                    dve.wait_ge(stored.of(E - 2), stored.at(E - 2))
                for j in range(J):
                    dve.wait_ge(attn_mm.sem, attn_mm.at(E, j + 1))
                    nc.vector.scalar_tensor_tensor(split(x3[:, E.odd, j, :]), conv_banks(j), b_out[:, j:j + 1],
                                                   split(x2[:, E.odd, j, :]), ALU.add, ALU.add,
                                                   accum_out=gn_in[:, 3, j:j + 1]).then_inc(x3_ready.sem, 1)

            def box_sums(F, steps):
                for n in steps:
                    if n == 0:
                        dve.wait_ge(x3pad_ready.sem, x3pad_ready.at(F, 1))
                        dve.wait_ge(setup_pool, SETUP_POOL)
                    else:
                        dve.wait_ge(box_step[0].sem, box_step[0].at(F, n))
                    dst, a, b = box_operands(0, n)
                    nc.vector.tensor_tensor(dst, a, b, ALU.add).then_inc(box_step[0].sem, 1)

            def make_x4(F):
                for j in range(J):
                    dve.wait_ge(box_step[j].sem, box_step[j].at(F))
                    x4 = x3[:, F.odd, j, :].rearrange("p (h w) -> p h w", w=W)
                    nc.vector.scalar_tensor_tensor(x4, x3pad[:, j, 1:1 + H, 1:1 + W], 1.0 / TAPS, x4, ALU.mult,
                                                   ALU.add).then_inc(x4_ready.sem, 1)

            def q_low(E):
                for n, (j, ms) in enumerate(QUADS):
                    cols = slice(ms[0] * TOK, (ms[-1] + 1) * TOK)
                    dve.wait_ge(qT_hi.sem, qT_hi.at(E, n + 1))
                    nc.vector.tensor_tensor(qT_parts[:, 1, j, cols], tile_ps[:, QT_BANK[n], 0:len(ms) * TOK],
                                            qT_parts[:, 0, j, cols].bitcast(F32), ALU.subtract).then_inc(qT_lo.sem, 1)

            def key_norms(E):
                dve.wait_ge(ksum_read.sem, ksum_read.at(E))
                nc.vector.tensor_scalar(k_inv[:, 0, :], k_norm[:], NORM_EPS, None, ALU.max).then_inc(kinv_step.sem, 1)
                dve.wait_ge(kinv_step.sem, kinv_step.at(E, 1))
                nc.vector.reciprocal(k_inv[:, 1, :], k_inv[:, 0, :]).then_inc(kinv_step.sem, 1)

            def attention_weights_low(E):
                dve.wait_ge(attn_hi.sem, attn_hi.at(E))
                for c in range(J):
                    nc.vector.scalar_tensor_tensor(attn_parts[:, 1, c, :], tile_ps[:, ATTN_BANK, c * C:(c + 1) * C],
                                                   k_inv[:, 1, c:c + 1], attn_parts[:, 0, c, :].bitcast(F32),
                                                   ALU.mult, ALU.subtract).then_inc(attn_lo.sem, 1)

            def x2_low(D):
                for j in range(J):
                    dve.wait_ge(xn2_hi.sem, xn2_hi.at(D, j + 1))
                    nc.vector.tensor_tensor(xn2_parts[:, 1, j, :], xn2[:, j, :], xn2_parts[:, 0, j, :].bitcast(F32),
                                            ALU.subtract).then_inc(xn2_lo.sem, 1)

            def reciprocal_sums(D):
                dve.wait_ge(k2_ready.sem, k2_ready.at(D))
                nc.vector.tensor_scalar(qk_rec[:], qk_sum[:], DIV_EPS, None, ALU.add).then_inc(rec_step.sem, 1)
                dve.wait_ge(rec_step.sem, rec_step.at(D, 1))
                nc.vector.reciprocal(qk_rec[:], qk_rec[:]).then_inc(rec_step.sem, 1)

            def q_scales(D):
                dve.wait_ge(q_root.sem, q_root.at(D))
                nc.vector.tensor_scalar(q_alpha[:, 0, :], q_norm[:], NORM_EPS, None, ALU.max).then_inc(alpha_step.sem, 1)
                dve.wait_ge(alpha_step.sem, alpha_step.at(D, 1))
                nc.vector.reciprocal(q_alpha[:, 1, :], q_alpha[:, 0, :]).then_inc(alpha_step.sem, 1)
                dve.wait_ge(alpha_step.sem, alpha_step.at(D, 2))
                nc.vector.scalar_tensor_tensor(q_alpha[:, 2, :], q_alpha[:, 1, :], float(HW) ** -0.5, qk_rec[:, 0, :],
                                               ALU.mult, ALU.mult).then_inc(alpha_step.sem, 1)

            def kx_low(E):
                dve.wait_ge(kx_hi.sem, kx_hi.at(E))
                nc.vector.tensor_tensor(kx_parts[:, 1], tile_ps[:, KX_BANK, :].rearrange("p (i c) -> p i c", i=J),
                                        kx_parts[:, 0].bitcast(F32), ALU.subtract).then_inc(kx_lo.sem, 1)

            def step(t):
                Z, A, B, C_, D, E, F = (t + 1 - n for n in range(STAGES))
                if A.started:
                    variances(A)
                    scales_shifts(A)
                if E.active:
                    kx_low(E)
                if A.active:
                    gate_logits(A)
                if B.active:
                    depthwise(B, slice(0, 1))
                if E.active:
                    q_low(E)
                    key_norms(E)
                if A.active:
                    sparsemax(A)
                if t.first:
                    setup_weights()
                if F.active:
                    box_sums(F, range(1))
                if E.active:
                    attention_weights_low(E)
                if B.active:
                    depthwise(B, slice(1, 3))
                if D.active:
                    x2_low(D)
                if C_.active:
                    h_mask(C_)
                if F.active:
                    box_sums(F, range(1, BOX_STEPS))
                if B.active:
                    depthwise(B, slice(3, 5))
                if E.active:
                    make_x3(E)
                if B.active:
                    depthwise(B, slice(5, 9))
                if B.active:
                    depthwise(B, slice(9, 10))
                if D.active:
                    reciprocal_sums(D)
                if B.active:
                    depthwise(B, slice(10, 13))
                if F.active:
                    make_x4(F)
                if C_.active:
                    make_x2(C_)
                if D.active:
                    q_scales(D)
                if B.active and not D.active:
                    depthwise(B, slice(13, None))
                if A.active:
                    make_x1(A)
                if B.active and D.active:
                    depthwise(B, slice(13, None))

            run(dve, step)

        @block.scalar
        def _(act):
            def setup():
                act.wait_ge(setup_dve, SETUP_BN)
                nc.scalar.activation(bn_shift[:], bn_tmp[:], ACT.Sqrt).then_inc(setup_act, 1)
                for k in range(3):
                    act.dma_start(bqk3[k:k + 1, :], bqk_parts[:, k, :]).then_inc(bias_moved, 16)

            act.wait_ge(setup_pool, SETUP_POOL)

            def junk_free(*writers):
                for img, count in writers:
                    if img.active:
                        act.wait_ge(count.sem, count.at(img))
                        return

            def deviations(A):
                act.wait_ge(gn.sem, gn.at(A, GN_VAR))
                nc.scalar.activation(gn_sd[:], gn_var[:], ACT.Sqrt).then_inc(gn_sqrt.sem, 1)

            def sum_squares(layer, img, source, ready):
                for j in range(J):
                    act.wait_ge(ready.sem, ready.at(img, j + 1))
                    nc.scalar.activation(junk[:, j * HW:(j + 1) * HW], source[:, j, :], ACT.Square,
                                         accum_out=gn_in[:, layer, 2 + j:3 + j]).then_inc(gn_sums[layer].sem, 1)

            def normalise(A, layer, outs, source, signal):
                act.wait_ge(gn.sem, gn.at(A))
                for j in range(J):
                    nc.scalar.activation(outs[j], source[j], ACT.Identity, bias=gn_s[:, layer, j:j + 1],
                                         scale=gn_r[:, layer, j:j + 1]).then_inc(signal.sem, 1)

            def normalise_x2(A, D):
                if (D - 1).active:
                    act.wait_ge(xT_mm.sem, xT_mm.at(D - 1))
                    act.wait_ge(xn2_lo.sem, xn2_lo.at(D - 1))
                normalise(A, 2, [xn2[:, j, :] for j in range(J)], [x2[:, D.odd, j, :] for j in range(J)], xn2_ready)

            def normalise_x3(A, F):
                if (F - 1).active:
                    act.wait_ge(x4_ready.sem, x4_ready.at(F - 1))
                normalise(A, 3, [x3pad[:, j, 1:1 + H, 1:1 + W] for j in range(J)],
                          [x3[:, F.odd, j, :].rearrange("p (h w) -> p h w", w=W) for j in range(J)], x3pad_ready)

            def normalise_x0(A, B):
                if B.active:
                    act.wait_ge(conv0_mm.sem, conv0_mm.at(B))
                normalise(A, 0, [xn0[:, j, :] for j in range(J)], [x0[:, A.odd, j, :] for j in range(J)], xn0_ready)

            def gated_experts(A):
                act.wait_ge(experts_loaded, EXPERTS_LOADED)
                act.wait_ge(gate_step.sem, gate_step.at(A))
                if (A - 1).active:
                    act.wait_ge(conv0_mm.sem, conv0_mm.at(A - 1))
                for k in range(1 + MIX_SLOTS):
                    nc.scalar.activation(mixed[:] if k == 0 else mix_tmp[:, k - 1, :],
                                         expert_sb[:, k, :], ACT.Identity,
                                         scale=gate[:, k:k + 1]).then_inc(mix_mul.sem, 1)

            def x0_sum(Z, n):
                func, first = ((ACT.Square, 2), (ACT.Identity, 0))[n // J]
                j = n % J
                if n == 0:
                    act.wait_ge(x_loaded.of(Z), x_loaded.at(Z))
                    if (Z - 1).active:
                        act.wait_ge(gate_step.sem, gate_step.at(Z - 1, 1))
                if n >= J:
                    act.wait_ge(gn_sums[0].sem, gn_sums[0].at(Z, n - J + 1))
                nc.scalar.activation(junk[:, j * HW:(j + 1) * HW], x0[:, Z.odd, j, :], func,
                                     accum_out=gn_in[:, 0, first + j:first + j + 1]).then_inc(gn_sums[0].sem, 1)

            def q_high(E):
                if (E - 1).active:
                    act.wait_ge(attn_mm.sem, attn_mm.at(E - 1))
                for n, (j, ms) in enumerate(QUADS):
                    act.wait_ge(qT_mm.sem, qT_mm.at(E, n + 1))
                    nc.scalar.copy(qT_parts[:, 0, j, ms[0] * TOK:(ms[-1] + 1) * TOK],
                                   tile_ps[:, QT_BANK[n], 0:len(ms) * TOK]).then_inc(qT_hi.sem, 1)

            def copy_tokens(D, banks):
                if (D - 1).active:
                    act.wait_ge(kx_mm.sem, kx_mm.at(D - 1))
                for b in banks:
                    ms = PAIRS[b]
                    act.wait_ge(xT_mm.sem, xT_mm.at(D, b + 1))
                    nc.scalar.copy(xT[:, ms[0]:ms[-1] + 1, :],
                                   tile_ps[0:TOK, XT_BANK[b], 0:len(ms) * C].rearrange("p (m c) -> p m c", c=C)
                                   ).then_inc(xT_ready.sem, 1)

            def key_sums(E):
                act.wait_ge(ksum_mm.sem, ksum_mm.at(E))
                nc.scalar.copy(k_row[:], tile_ps[0:1, KSUM_BANK, 0:C]).then_inc(ksum_read.sem, 1)
                nc.scalar.activation(k_norm[:], tile_ps[:, KSUM_BANK, C:C + J], ACT.Sqrt).then_inc(ksum_read.sem, 1)

            def attention_weights_high(E):
                act.wait_ge(attn_w_mm.sem, attn_w_mm.at(E))
                act.wait_ge(kinv_step.sem, kinv_step.at(E))
                for c in range(J):
                    nc.scalar.activation(attn_parts[:, 0, c, :], tile_ps[:, ATTN_BANK, c * C:(c + 1) * C],
                                         ACT.Identity, scale=k_inv[:, 1, c:c + 1]).then_inc(attn_hi.sem, 1)

            def x2_high(D):
                act.wait_ge(xn2_ready.sem, xn2_ready.at(D))
                if (D - 1).active:
                    act.wait_ge(value_mm.sem, value_mm.at(D - 1))
                for j in range(J):
                    nc.scalar.copy(xn2_parts[:, 0, j, :], xn2[:, j, :]).then_inc(xn2_hi.sem, 1)

            def relu_h(B, j):
                act.wait_ge(dw_step[j].sem, dw_step[j].at(B))
                nc.scalar.activation(h[:, B.odd, j, :], h[:, B.odd, j, :], ACT.Relu, bias=bn_shift[:, 0, j:j + 1],
                                     scale=bn_scale[:, 0, j:j + 1]).then_inc(h_ready.sem, 1)

            def relu_y(C_, j):
                if (C_ - 2).active:
                    act.wait_ge(x3_ready.sem, x3_ready.at(C_ - 2))
                act.wait_ge(pw_mm.sem, pw_mm.at(C_, j + 1))
                nc.scalar.activation(split(x2[:, C_.odd, j, :]), conv_banks(j), ACT.Relu,
                                     bias=bn_shift[:, 1, j:j + 1],
                                     scale=bn_scale[:, 1, j:j + 1]).then_inc(y_ready.sem, 1)

            def square_qk(D, m):
                if m == 0 and (D - 1).active:
                    act.wait_ge(qT_mm.sem, qT_mm.at(D - 1))
                    act.wait_ge(kx_mm.sem, kx_mm.at(D - 1))
                    act.wait_ge(ksum_step.sem, ksum_step.at(D - 1))
                act.wait_ge(qk_mm.sem, qk_mm.at(D, m + 1))
                bank = tile_ps[0:TOK, QK_BANK[m], :]
                nc.scalar.activation(q2[:, m, :], bank[:, 0:C], ACT.Square,
                                     accum_out=qk_sum[:, 0, m:m + 1]).then_inc(q2_ready.sem, 1)
                nc.scalar.activation(k2[:, m, :], bank[:, C:2 * C], ACT.Square,
                                     accum_out=qk_sum[:, 1, m:m + 1]).then_inc(k2_ready.sem, 1)

            def q_norms(D):
                act.wait_ge(rec_step.sem, rec_step.at(D))
                for m in range(M):
                    nc.scalar.activation(junk[0:TOK, m * C:(m + 1) * C], q2[:, m, :], ACT.Square,
                                         scale=qk_rec[:, 0, m:m + 1],
                                         accum_out=q_nsq[:, m:m + 1]).then_inc(q4_ready.sem, 1)
                act.wait_ge(q4_ready.sem, q4_ready.at(D))
                nc.scalar.activation(q_norm[:], q_nsq[:], ACT.Sqrt).then_inc(q_root.sem, 1)

            def scale_q(D):
                act.wait_ge(alpha_step.sem, alpha_step.at(D))
                for m in range(M):
                    nc.scalar.activation(q2[:, m, :], q2[:, m, :], ACT.Identity,
                                         scale=q_alpha[:, 2, m:m + 1]).then_inc(qa_ready.sem, 1)

            def kx_high(E):
                act.wait_ge(kx_mm.sem, kx_mm.at(E))
                if (E - 1).active:
                    act.wait_ge(attn_w_mm.sem, attn_w_mm.at(E - 1))
                nc.scalar.copy(kx_parts[:, 0], tile_ps[:, KX_BANK, :].rearrange("p (i c) -> p i c", i=J)
                               ).then_inc(kx_hi.sem, 1)

            def step(t):
                Z, A, B, C_, D, E, F = (t + 1 - n for n in range(STAGES))
                if A.started:
                    deviations(A)
                if E.active:
                    kx_high(E)
                if D.active:
                    normalise_x2(A, D)
                if E.active:
                    q_high(E)
                    key_sums(E)
                if D.active:
                    copy_tokens(D, range(1))
                if F.active:
                    normalise_x3(A, F)
                if E.active:
                    attention_weights_high(E)
                if D.active:
                    copy_tokens(D, range(1, 3))
                    x2_high(D)
                if C_.active:
                    relu_h(C_, 1)
                if D.active:
                    copy_tokens(D, range(3, 4))
                if A.active:
                    normalise_x0(A, B)
                if A.active:
                    gated_experts(A)
                if t.first:
                    setup()
                for m in range(M):
                    if D.active:
                        square_qk(D, m)
                    if Z.active and 0 < m <= 2 * J:
                        x0_sum(Z, m - 1)
                if E.active:
                    junk_free((Z, gn_sums[0]))
                    sum_squares(3, E, x3[:, E.odd], x3_ready)
                if C_.active:
                    relu_y(C_, 0)
                if C_.active:
                    relu_y(C_, 1)
                if D.active:
                    junk_free((E, gn_sums[3]), (Z, gn_sums[0]))
                    q_norms(D)
                if C_.active:
                    junk_free((D, q4_ready), (E, gn_sums[3]), (Z, gn_sums[0]))
                    sum_squares(2, C_, x2[:, C_.odd], x2_ready)
                if t.first:
                    act.wait_ge(setup_dve, SETUP_DVE)
                if A.active:
                    junk_free((C_, gn_sums[2]), (Z, gn_sums[0]))
                    sum_squares(1, A, x1[:, A.odd], x1_ready)
                if D.active:
                    scale_q(D)
                if B.active:
                    relu_h(B, 0)

            run(act, step)

        @block.gpsimd
        def _(pool):
            nc.gpsimd.memset(ones[:], 1.0).then_inc(setup_pool, 1)
            nc.gpsimd.memset(ones3[:], 1.0).then_inc(setup_pool, 1)
            nc.gpsimd.memset(xpad[:], 0.0).then_inc(setup_pool, 1)
            nc.gpsimd.memset(x3pad[:], 0.0).then_inc(setup_pool, 1)
            nc.gpsimd.memset(row_sums[:], 0.0).then_inc(setup_pool, 1)
            nc.gpsimd.memset(gn_in[:], 0.0).then_inc(setup_pool, 1)

            def normalise_x1(A, B, C_):
                pool.wait_ge(setup_pool, SETUP_POOL)
                pool.wait_ge(gn.sem, gn.at(A))
                if C_.active:
                    for count in dw_step:
                        pool.wait_ge(count.sem, count.at(C_))
                hold(pool, "pool")
                for j in range(J):
                    nc.gpsimd.tensor_scalar(xpad[:, j, 1:1 + H, 1:1 + W],
                                            x1[:, B.odd, j, :].rearrange("p (h w) -> p h w", w=W),
                                            gn_r[:, 1, j:j + 1], gn_s[:, 1, j:j + 1], ALU.mult,
                                            ALU.add).then_inc(xpad_ready.sem, 1)

            def box_sums(F):
                pool.wait_ge(x3pad_ready.sem, x3pad_ready.at(F))
                for n in range(BOX_STEPS):
                    if n:
                        pool.wait_ge(box_step[1].sem, box_step[1].at(F, n))
                    nc.gpsimd.tensor_tensor(*box_operands(1, n), ALU.add).then_inc(box_step[1].sem, 1)

            def mask_weights(C_):
                if (C_ - 1).active:
                    pool.wait_ge(pw_mm.sem, pw_mm.at(C_ - 1))
                pool.wait_ge(w_loaded, LOADED)
                pool.wait_ge(hmask_step.sem, hmask_step.at(C_))
                hold(pool, "pool")
                for j in range(J):
                    nc.gpsimd.tensor_scalar(pw_masked[:, j, :], pw_sb[:, j, :], hmask[:, j:j + 1], 0.0, ALU.mult,
                                            ALU.add).then_inc(pw_masked_ready.sem, 1)

            def mix(A):
                for k in range(1, EXPERTS):
                    slot = mix_tmp[:, (k - 1) % MIX_SLOTS, :]
                    rest = k - MIX_SLOTS
                    if rest > 0:
                        pool.wait_ge(mix_step.sem, mix_step.at(A, rest))
                        hold(pool, "pool")
                        nc.gpsimd.tensor_scalar(slot, expert_sb[:, k, :], gate[:, k:k + 1], 0.0, ALU.mult,
                                                ALU.add).then_inc(mix_mul_rest.sem, 1)
                        pool.wait_ge(mix_mul_rest.sem, mix_mul_rest.at(A, rest))
                    else:
                        pool.wait_ge(mix_mul.sem, mix_mul.at(A, k + 1))
                    if k > 1:
                        pool.wait_ge(mix_step.sem, mix_step.at(A, k - 1))
                    nc.gpsimd.tensor_tensor(mixed[:], mixed[:], slot, ALU.add).then_inc(mix_step.sem, 1)

            def scale_k(D):
                pool.wait_ge(rec_step.sem, rec_step.at(D))
                hold(pool, "pool")
                for m in range(M):
                    nc.gpsimd.tensor_scalar(k2[:, m, :], k2[:, m, :], qk_rec[:, 1, m:m + 1], 0.0, ALU.mult,
                                            ALU.add).then_inc(kn_ready.sem, 1)

            def sum_k(D):
                if (D - 1).active:
                    pool.wait_ge(ksum_mm.sem, ksum_mm.at(D - 1))
                done = 0
                for m in range(M):
                    pool.wait_ge(kn_ready.sem, kn_ready.at(D, m + 1))
                    if m == 0:
                        nc.gpsimd.tensor_tensor(ksum[:, 1, :], k2[:, 0, :], k2[:, 0, :], ALU.mult).then_inc(
                            ksum_step.sem, 1)
                        done += 1
                        continue
                    if m >= 3:
                        pool.wait_ge(ksum_step.sem, ksum_step.at(D, 3 * (m - 2) + 1))
                    nc.gpsimd.tensor_tensor(ksq[:, m % 2, :], k2[:, m, :], k2[:, m, :], ALU.mult).then_inc(
                        ksum_step.sem, 1)
                    a = k2[:, 0, :] if m == 1 else ksum[:, 0, :]
                    nc.gpsimd.tensor_tensor(ksum[:, 0, :], a, k2[:, m, :], ALU.add).then_inc(ksum_step.sem, 1)
                    done += 2
                    pool.wait_ge(ksum_step.sem, ksum_step.at(D, done))
                    nc.gpsimd.tensor_tensor(ksum[:, 1, :], ksum[:, 1, :], ksq[:, m % 2, :], ALU.add).then_inc(
                        ksum_step.sem, 1)
                    done += 1

            def step(t):
                Z, A, B, C_, D, E, F = (t + 1 - n for n in range(STAGES))
                if B.active:
                    normalise_x1(A, B, C_)
                if F.active:
                    box_sums(F)
                if C_.active:
                    mask_weights(C_)
                if A.active:
                    mix(A)
                if D.active:
                    scale_k(D)
                    sum_k(D)

            run(pool, step)


SETUP_PARTS = 12 + 6 + 5
SETUP_BN = SETUP_PARTS + 2
SETUP_DVE = SETUP_BN + 10 + 2 + 2 + 2
SETUP_POOL = 6
QT_BANK, KSUM_BANK, ATTN_BANK = [0, 1, 2, 0], 1, 2
XT_BANK, QK_BANK, KX_BANK = [0, 1, 0, 1], [(m + 2) % 3 for m in range(M)], 2


def kernel(x, L0_conv_gate_w, L0_conv_gate_b, L0_conv_expert_w, L1_conv_dw_w, L1_conv_dw_b, L1_conv_bn1_g,
           L1_conv_bn1_b, L1_conv_bn1_m, L1_conv_bn1_v, L1_conv_pw_w, L1_conv_pw_b, L1_conv_bn2_g, L1_conv_bn2_b,
           L1_conv_bn2_m, L1_conv_bn2_v, L2_conv_Wqkv, L2_conv_bqkv, L2_conv_Wln, L2_conv_bln):
    import numpy as np
    import concourse.bacc as bacc
    from concourse.bass_utils import run_bass_kernel_spmd

    c = np.arange(P)
    group_mean = ((c[:, None] // GROUP) == (c[None, :] // GROUP)).astype(np.float32) / (GROUP * HW)
    per_channel = {
        "dw_b": L1_conv_dw_b, "pw_b": L1_conv_pw_b, "b_ln": L2_conv_bln, "b_v": np.asarray(L2_conv_bqkv)[2 * C:],
        "bn1_g": L1_conv_bn1_g, "bn1_b": L1_conv_bn1_b, "bn1_m": L1_conv_bn1_m, "bn1_v": L1_conv_bn1_v,
        "bn2_g": L1_conv_bn2_g, "bn2_b": L1_conv_bn2_b, "bn2_m": L1_conv_bn2_m, "bn2_v": L1_conv_bn2_v,
    }
    arrays = {
        "x": x,
        "gate_wT": np.asarray(L0_conv_gate_w).T,
        "gate_b": L0_conv_gate_b,
        "expert_wT": np.asarray(L0_conv_expert_w).transpose(0, 2, 1),
        "dw_w": L1_conv_dw_w,
        "channel_params": np.stack([np.asarray(per_channel[name]).reshape(J, P) for name in PARAMS]).transpose(2, 0, 1),
        "pw_wT": np.asarray(L1_conv_pw_w)[:, :, 0, 0].T,
        "w_qk": np.asarray(L2_conv_Wqkv)[:, :2 * C],
        "b_qk": np.asarray(L2_conv_bqkv)[:2 * C],
        "w_vT": np.asarray(L2_conv_Wqkv)[:, 2 * C:].T,
        "w_ln": L2_conv_Wln,
        "group_mean": group_mean,
        "ident": np.eye(P, dtype=np.float32),
    }
    arrays = {name: np.ascontiguousarray(a) for name, a in arrays.items()}
    nc = bacc.Bacc("TRN2", target_bir_lowering=False, num_devices=1)
    t = {name: nc.dram_tensor(name, a.shape, mybir.dt.from_np(a.dtype), kind="ExternalInput").ap()
         for name, a in arrays.items()}
    out = nc.dram_tensor("out", (IMAGES, C, H, W), F32, kind="ExternalOutput").ap()
    build(nc, out=out, **t)
    r = run_bass_kernel_spmd(nc, [arrays], core_ids=[0])
    return r.results[0]["out"]
```
